# Optimizing a Trainium2 kernel written in Bass

```python
import numpy as np
import jax
import jax.numpy as jnp

def _softmax(x, axis=-1):
    return jax.nn.softmax(x, axis=axis)

def _gelu(x):
    return jax.nn.gelu(x, approximate=True)

def _silu(x):
    return jax.nn.silu(x)

def _sigmoid(x):
    return jax.nn.sigmoid(x)

def _layernorm(x, axis=-1, eps=1e-05):
    m = jnp.mean(x, axis=axis, keepdims=True)
    v = jnp.var(x, axis=axis, keepdims=True)
    return (x - m) / jnp.sqrt(v + eps)

def _scatter_add(tgt, idx, src, axis=0):
    return tgt.at[idx].add(src)

def _segment_sum(src, seg, n):
    return jax.ops.segment_sum(src, seg, n)
kernel_name = 'mk_gnn_preln_d4_gnn_r32_dbda90'

def setup_inputs(seed: int=0):
    np.random.seed(seed)
    _w = jnp.asarray

    def _rec_inputs():
        import jax
        import jax.numpy as jnp
        _gk = jax.random.key(seed)
        x = -0.0005207 + 1.001 * jax.random.normal(jax.random.fold_in(_gk, 1), (128, 512), jnp.float32)
        src = jax.random.randint(jax.random.fold_in(_gk, 2), (4096,), 0, 128, jnp.int32)
        dst = jnp.minimum((128 * jax.random.uniform(jax.random.fold_in(_gk, 3), (4096,)) ** 2.0).astype(jnp.int32), 4095)
        _o = jnp.argsort(dst, stable=True)
        src = src[_o]
        dst = dst[_o]
        edge_attr_4 = 0.00171547 + 0.999346 * jax.random.normal(jax.random.fold_in(_gk, 12), (4096, 4), jnp.float32)
        edge_attr_8 = 0.000126197 + 0.999763 * jax.random.normal(jax.random.fold_in(_gk, 13), (4096, 8), jnp.float32)
        return (x, src, dst, edge_attr_4, edge_attr_8)
    x, src, dst, edge_attr_4, edge_attr_8 = _rec_inputs()

    def _L0_gnn_setup():
        import jax, jax.numpy as jnp
        import numpy as np
        N, D, H, E = (128, 512, 8, 4096)
        DH = D // H
        EPS = 1e-05
        NEG = -1000000000.0

        def layer_norm(x, w, b):
            m = jnp.mean(x, axis=-1, keepdims=True)
            v = jnp.mean((x - m) ** 2, axis=-1, keepdims=True)
            return (x - m) * jax.lax.rsqrt(v + EPS) * w + b
        key = jax.random.key(seed)
        ks = jax.random.split(key, 10)
        s = 0.02
        return {'x': jax.random.normal(ks[0], (N, D), dtype=jnp.float32), 'edge_index': jax.random.randint(ks[1], (2, E), 0, N, dtype=jnp.int64), 'ln1_w': jnp.ones((D,), jnp.float32), 'ln1_b': jnp.zeros((D,), jnp.float32), 'w_in': jax.random.normal(ks[2], (3 * D, D), jnp.float32) * s, 'b_in': jnp.zeros((3 * D,), jnp.float32), 'w_out': jax.random.normal(ks[3], (D, D), jnp.float32) * s, 'b_out': jnp.zeros((D,), jnp.float32), 'ln2_w': jnp.ones((D,), jnp.float32), 'ln2_b': jnp.zeros((D,), jnp.float32), 'w1': jax.random.normal(ks[4], (4 * D, D), jnp.float32) * s, 'b1': jnp.zeros((4 * D,), jnp.float32), 'w2': jax.random.normal(ks[5], (D, 4 * D), jnp.float32) * s, 'b2': jnp.zeros((D,), jnp.float32)}
    _L0_gnn_all = _L0_gnn_setup()
    _L0_gnn_in = {k: v for k, v in _L0_gnn_all.items() if k in ('ln1_w', 'ln1_b', 'w_in', 'b_in', 'w_out', 'b_out', 'ln2_w', 'ln2_b', 'w1', 'b1', 'w2', 'b2')}
    del _L0_gnn_all

    def _L1_gnn_setup():
        import jax, jax.numpy as jnp
        import numpy as np
        MUL = 128
        N_NODES = 10000
        N_EDGES = 5000
        R_BASIS = 8
        HIDDEN = 64
        W_NUMEL = 4 * MUL
        SQRT3 = 3.0 ** 0.5
        SILU_2MOM = 1.679177
        AVG_NUM_NEIGHBORS = 10.0

        def _lin_irreps(x0, x1, W0, W1):
            y0 = x0 @ W0 / jnp.sqrt(jnp.float32(W0.shape[0]))
            y1 = jnp.einsum('num,uv->nvm', x1, W1) / jnp.sqrt(jnp.float32(W1.shape[0]))
            return (y0, y1)

        def _forward(node_feats, edge_attrs, edge_feats, edge_index, W_up0, W_up1, W_mlp1, W_mlp2, W_mlp3, W_mlp4, W_out0, W_out1):
            num_nodes = node_feats.shape[0]
            sender, receiver = (edge_index[0], edge_index[1])
            x0 = node_feats[:, :MUL]
            x1 = node_feats[:, MUL:].reshape(num_nodes, MUL, 3)
            x0, x1 = _lin_irreps(x0, x1, W_up0, W_up1)
            h = edge_feats
            for W in (W_mlp1, W_mlp2, W_mlp3):
                h = SILU_2MOM * jax.nn.silu(h @ W / jnp.sqrt(jnp.float32(W.shape[0])))
            tpw = h @ W_mlp4 / jnp.sqrt(jnp.float32(W_mlp4.shape[0]))
            w1, w2, w3, w4 = jnp.split(tpw, 4, axis=-1)
            s0 = x0[sender]
            s1 = x1[sender]
            y0 = edge_attrs[:, 0:1]
            y1 = edge_attrs[:, 1:4]
            p1 = w1 * s0 * y0
            p2 = (w2 * s0)[:, :, None] * y1[:, None, :]
            p3 = w3[:, :, None] * s1 * y0[:, None, :]
            p4 = w4 * jnp.einsum('eum,em->eu', s1, y1) / SQRT3
            m0 = jnp.concatenate([p1, p4], axis=-1)
            m1 = jnp.concatenate([p2, p3], axis=1)
            msg0 = jax.ops.segment_sum(m0, receiver, num_segments=num_nodes)
            msg1 = jax.ops.segment_sum(m1, receiver, num_segments=num_nodes)
            o0, o1 = _lin_irreps(msg0, msg1, W_out0, W_out1)
            out = jnp.concatenate([o0, o1.reshape(num_nodes, 3 * MUL)], axis=-1)
            return out / AVG_NUM_NEIGHBORS
        key = jax.random.key(seed)
        ks = jax.random.split(key, 12)
        rn = lambda k, s: jax.random.normal(k, s, dtype=jnp.float32)
        return {'node_feats': rn(ks[0], (N_NODES, 4 * MUL)), 'edge_attrs': rn(ks[1], (N_EDGES, 4)), 'edge_feats': rn(ks[2], (N_EDGES, R_BASIS)), 'edge_index': jax.random.randint(ks[3], (2, N_EDGES), 0, N_NODES), 'W_up0': rn(ks[4], (MUL, MUL)), 'W_up1': rn(ks[5], (MUL, MUL)), 'W_mlp1': rn(ks[6], (R_BASIS, HIDDEN)), 'W_mlp2': rn(ks[7], (HIDDEN, HIDDEN)), 'W_mlp3': rn(ks[8], (HIDDEN, HIDDEN)), 'W_mlp4': rn(ks[9], (HIDDEN, W_NUMEL)), 'W_out0': rn(ks[10], (2 * MUL, MUL)), 'W_out1': rn(ks[11], (2 * MUL, MUL))}
    _L1_gnn_all = _L1_gnn_setup()
    _L1_gnn_in = {k: v for k, v in _L1_gnn_all.items() if k in ('W_up0', 'W_up1', 'W_mlp1', 'W_mlp2', 'W_mlp3', 'W_mlp4', 'W_out0', 'W_out1')}
    del _L1_gnn_all

    def _L2_gnn_setup():
        import jax, jax.numpy as jnp
        import numpy as np
        N_NODES = 10000
        N_EDGES = 5000
        D_IN = 512
        D_HID = 1024
        key = jax.random.key(seed)
        ks = jax.random.split(key, 8)
        feat = jax.random.normal(ks[0], (N_NODES, D_IN), dtype=jnp.float32)
        W1 = jax.random.normal(ks[1], (D_IN, D_HID), dtype=jnp.float32) * (1.0 / np.sqrt(D_IN))
        b1 = jnp.zeros((D_HID,), dtype=jnp.float32)
        W2 = jax.random.normal(ks[2], (D_HID, D_IN), dtype=jnp.float32) * (1.0 / np.sqrt(D_HID))
        b2 = jnp.zeros((D_IN,), dtype=jnp.float32)
        eps = jnp.zeros((1,), dtype=jnp.float32)
        src = jax.random.randint(ks[3], (N_EDGES,), 0, N_NODES, dtype=jnp.int32)
        dst = jax.random.randint(ks[4], (N_EDGES,), 0, N_NODES, dtype=jnp.int32)
        return {'feat': feat, 'W1': W1, 'b1': b1, 'W2': W2, 'b2': b2, 'eps': eps, 'src': src, 'dst': dst}
    _L2_gnn_all = _L2_gnn_setup()
    _L2_gnn_in = {k: v for k, v in _L2_gnn_all.items() if k in ('W1', 'b1', 'W2', 'b2', 'eps')}
    del _L2_gnn_all

    def _L3_gnn_setup():
        import jax, jax.numpy as jnp
        import numpy as np
        N = 50000
        E = 12500
        D_IN = 512
        D_HID = 64
        D_OUT = 512
        key = jax.random.key(seed)
        k1, k2, k3, k4 = jax.random.split(key, 4)
        x = jax.random.normal(k1, (N, D_IN), dtype=jnp.float32)
        edge_index = jax.random.randint(k2, (2, E), 0, N, dtype=jnp.int64)
        W1 = jax.random.normal(k3, (D_IN, D_HID), dtype=jnp.float32) * (1.0 / np.sqrt(D_IN))
        b1 = jnp.zeros((D_HID,), dtype=jnp.float32)
        W2 = jax.random.normal(k4, (D_HID, D_OUT), dtype=jnp.float32) * (1.0 / np.sqrt(D_HID))
        b2 = jnp.zeros((D_OUT,), dtype=jnp.float32)
        return {'x': x, 'edge_index': edge_index, 'W1': W1, 'b1': b1, 'W2': W2, 'b2': b2}
    _L3_gnn_all = _L3_gnn_setup()
    _L3_gnn_in = {k: v for k, v in _L3_gnn_all.items() if k in ('W1', 'b1', 'W2', 'b2')}
    del _L3_gnn_all
    return {'x': x, 'src': src, 'dst': dst, 'edge_attr_4': edge_attr_4, 'edge_attr_8': edge_attr_8, 'L0_gnn_ln1_w': _L0_gnn_in['ln1_w'], 'L0_gnn_ln1_b': _L0_gnn_in['ln1_b'], 'L0_gnn_w_in': _L0_gnn_in['w_in'], 'L0_gnn_b_in': _L0_gnn_in['b_in'], 'L0_gnn_w_out': _L0_gnn_in['w_out'], 'L0_gnn_b_out': _L0_gnn_in['b_out'], 'L0_gnn_ln2_w': _L0_gnn_in['ln2_w'], 'L0_gnn_ln2_b': _L0_gnn_in['ln2_b'], 'L0_gnn_w1': _L0_gnn_in['w1'], 'L0_gnn_b1': _L0_gnn_in['b1'], 'L0_gnn_w2': _L0_gnn_in['w2'], 'L0_gnn_b2': _L0_gnn_in['b2'], 'L1_gnn_W_up0': _L1_gnn_in['W_up0'], 'L1_gnn_W_up1': _L1_gnn_in['W_up1'], 'L1_gnn_W_mlp1': _L1_gnn_in['W_mlp1'], 'L1_gnn_W_mlp2': _L1_gnn_in['W_mlp2'], 'L1_gnn_W_mlp3': _L1_gnn_in['W_mlp3'], 'L1_gnn_W_mlp4': _L1_gnn_in['W_mlp4'], 'L1_gnn_W_out0': _L1_gnn_in['W_out0'], 'L1_gnn_W_out1': _L1_gnn_in['W_out1'], 'L2_gnn_W1': _L2_gnn_in['W1'], 'L2_gnn_b1': _L2_gnn_in['b1'], 'L2_gnn_W2': _L2_gnn_in['W2'], 'L2_gnn_b2': _L2_gnn_in['b2'], 'L2_gnn_eps': _L2_gnn_in['eps'], 'L3_gnn_W1': _L3_gnn_in['W1'], 'L3_gnn_b1': _L3_gnn_in['b1'], 'L3_gnn_W2': _L3_gnn_in['W2'], 'L3_gnn_b2': _L3_gnn_in['b2']}

def reference(x, src, dst, edge_attr_4, edge_attr_8, L0_gnn_ln1_w, L0_gnn_ln1_b, L0_gnn_w_in, L0_gnn_b_in, L0_gnn_w_out, L0_gnn_b_out, L0_gnn_ln2_w, L0_gnn_ln2_b, L0_gnn_w1, L0_gnn_b1, L0_gnn_w2, L0_gnn_b2, L1_gnn_W_up0, L1_gnn_W_up1, L1_gnn_W_mlp1, L1_gnn_W_mlp2, L1_gnn_W_mlp3, L1_gnn_W_mlp4, L1_gnn_W_out0, L1_gnn_W_out1, L2_gnn_W1, L2_gnn_b1, L2_gnn_W2, L2_gnn_b2, L2_gnn_eps, L3_gnn_W1, L3_gnn_b1, L3_gnn_W2, L3_gnn_b2):
    import jax
    import jax.numpy as jnp

    def _L0_gnn_ref(x, edge_index, ln1_w, ln1_b, w_in, b_in, w_out, b_out, ln2_w, ln2_b, w1, b1, w2, b2):
        import jax, jax.numpy as jnp
        import numpy as np
        N, D, H, E = (128, 512, 8, 4096)
        DH = D // H
        EPS = 1e-05
        NEG = -1000000000.0

        def layer_norm(x, w, b):
            m = jnp.mean(x, axis=-1, keepdims=True)
            v = jnp.mean((x - m) ** 2, axis=-1, keepdims=True)
            return (x - m) * jax.lax.rsqrt(v + EPS) * w + b
        n = x.shape[0]
        adj = jnp.zeros((n, n), dtype=bool)
        adj = adj.at[edge_index[0], edge_index[1]].set(True)
        adj = adj.at[jnp.arange(n), jnp.arange(n)].set(True)
        add_mask = jnp.where(adj, 0.0, NEG).astype(x.dtype)
        xn = layer_norm(x, ln1_w, ln1_b)
        qkv = xn @ w_in.T + b_in
        q, k, v = jnp.split(qkv, 3, axis=-1)
        q = q.reshape(n, H, DH).transpose(1, 0, 2)
        k = k.reshape(n, H, DH).transpose(1, 0, 2)
        v = v.reshape(n, H, DH).transpose(1, 0, 2)
        scores = jnp.einsum('hqd,hkd->hqk', q, k) / jnp.sqrt(jnp.asarray(DH, x.dtype))
        scores = scores + add_mask[None]
        attn = jax.nn.softmax(scores, axis=-1)
        o = jnp.einsum('hqk,hkd->hqd', attn, v)
        o = o.transpose(1, 0, 2).reshape(n, D)
        attn_out = o @ w_out.T + b_out
        x = x + attn_out
        xm = layer_norm(x, ln2_w, ln2_b)
        mlp = jax.nn.relu(xm @ w1.T + b1) @ w2.T + b2
        return x + mlp

    def _L1_gnn_ref(node_feats, edge_attrs, edge_feats, edge_index, W_up0, W_up1, W_mlp1, W_mlp2, W_mlp3, W_mlp4, W_out0, W_out1):
        import jax, jax.numpy as jnp
        import numpy as np
        MUL = 128
        N_NODES = 10000
        N_EDGES = 5000
        R_BASIS = 8
        HIDDEN = 64
        W_NUMEL = 4 * MUL
        SQRT3 = 3.0 ** 0.5
        SILU_2MOM = 1.679177
        AVG_NUM_NEIGHBORS = 10.0

        def _lin_irreps(x0, x1, W0, W1):
            y0 = x0 @ W0 / jnp.sqrt(jnp.float32(W0.shape[0]))
            y1 = jnp.einsum('num,uv->nvm', x1, W1) / jnp.sqrt(jnp.float32(W1.shape[0]))
            return (y0, y1)

        def _forward(node_feats, edge_attrs, edge_feats, edge_index, W_up0, W_up1, W_mlp1, W_mlp2, W_mlp3, W_mlp4, W_out0, W_out1):
            num_nodes = node_feats.shape[0]
            sender, receiver = (edge_index[0], edge_index[1])
            x0 = node_feats[:, :MUL]
            x1 = node_feats[:, MUL:].reshape(num_nodes, MUL, 3)
            x0, x1 = _lin_irreps(x0, x1, W_up0, W_up1)
            h = edge_feats
            for W in (W_mlp1, W_mlp2, W_mlp3):
                h = SILU_2MOM * jax.nn.silu(h @ W / jnp.sqrt(jnp.float32(W.shape[0])))
            tpw = h @ W_mlp4 / jnp.sqrt(jnp.float32(W_mlp4.shape[0]))
            w1, w2, w3, w4 = jnp.split(tpw, 4, axis=-1)
            s0 = x0[sender]
            s1 = x1[sender]
            y0 = edge_attrs[:, 0:1]
            y1 = edge_attrs[:, 1:4]
            p1 = w1 * s0 * y0
            p2 = (w2 * s0)[:, :, None] * y1[:, None, :]
            p3 = w3[:, :, None] * s1 * y0[:, None, :]
            p4 = w4 * jnp.einsum('eum,em->eu', s1, y1) / SQRT3
            m0 = jnp.concatenate([p1, p4], axis=-1)
            m1 = jnp.concatenate([p2, p3], axis=1)
            msg0 = jax.ops.segment_sum(m0, receiver, num_segments=num_nodes)
            msg1 = jax.ops.segment_sum(m1, receiver, num_segments=num_nodes)
            o0, o1 = _lin_irreps(msg0, msg1, W_out0, W_out1)
            out = jnp.concatenate([o0, o1.reshape(num_nodes, 3 * MUL)], axis=-1)
            return out / AVG_NUM_NEIGHBORS
        return _forward(node_feats, edge_attrs, edge_feats, edge_index, W_up0, W_up1, W_mlp1, W_mlp2, W_mlp3, W_mlp4, W_out0, W_out1)

    def _L2_gnn_ref(feat, W1, b1, W2, b2, eps, src, dst):
        import jax, jax.numpy as jnp
        import numpy as np
        N_NODES = 10000
        N_EDGES = 5000
        D_IN = 512
        D_HID = 1024
        msgs = feat[src]
        neigh = jax.ops.segment_sum(msgs, dst, num_segments=feat.shape[0])
        rst = (1.0 + eps[0]) * feat + neigh
        h = jnp.maximum(rst @ W1 + b1, 0.0)
        h = h @ W2 + b2
        return h + feat

    def _L3_gnn_ref(x, edge_index, W1, b1, W2, b2):
        import jax, jax.numpy as jnp
        import numpy as np
        N = 50000
        E = 12500
        D_IN = 512
        D_HID = 64
        D_OUT = 512
        h = jax.nn.relu(x @ W1 + b1) @ W2 + b2
        row, col = (edge_index[0], edge_index[1])
        agg = jax.ops.segment_sum(h[col], row, num_segments=h.shape[0])
        return h + agg
    edge_index = jnp.stack([src, dst])
    h = jnp.maximum(_layernorm(x, axis=-1), 0.0)
    x = x + _L0_gnn_ref(h, edge_index, L0_gnn_ln1_w, L0_gnn_ln1_b, L0_gnn_w_in, L0_gnn_b_in, L0_gnn_w_out, L0_gnn_b_out, L0_gnn_ln2_w, L0_gnn_ln2_b, L0_gnn_w1, L0_gnn_b1, L0_gnn_w2, L0_gnn_b2)
    h = jnp.maximum(_layernorm(x, axis=-1), 0.0)
    x = x + _L1_gnn_ref(h, edge_attr_4, edge_attr_8, edge_index, L1_gnn_W_up0, L1_gnn_W_up1, L1_gnn_W_mlp1, L1_gnn_W_mlp2, L1_gnn_W_mlp3, L1_gnn_W_mlp4, L1_gnn_W_out0, L1_gnn_W_out1)
    h = jnp.maximum(_layernorm(x, axis=-1), 0.0)
    x = x + _L2_gnn_ref(h, L2_gnn_W1, L2_gnn_b1, L2_gnn_W2, L2_gnn_b2, L2_gnn_eps, src, dst)
    h = jnp.maximum(_layernorm(x, axis=-1), 0.0)
    x = x + _L3_gnn_ref(h, edge_index, L3_gnn_W1, L3_gnn_b1, L3_gnn_W2, L3_gnn_b2)
    return x

_drawn_inputs = setup_inputs


def setup_inputs(seed=0):
    import zlib

    import numpy as np

    out = dict(_drawn_inputs(seed))
    spreads = {'L0_gnn_ln1_w': (1.0, 0.6),
     'L0_gnn_ln1_b': (0.0, 0.58),
     'L0_gnn_b_in': (0.0, 0.276),
     'L0_gnn_b_out': (0.0, 0.1),
     'L0_gnn_ln2_w': (1.0, 0.6),
     'L0_gnn_ln2_b': (0.0, 0.616),
     'L0_gnn_b1': (0.0, 0.328),
     'L0_gnn_b2': (0.0, 0.1),
     'L2_gnn_b1': (0.0, 0.8),
     'L2_gnn_b2': (0.0, 0.8),
     'L3_gnn_b1': (0.0, 0.1),
     'L3_gnn_b2': (0.0, 0.1)}
    factors = {'L0_gnn_w_in': 2.725}
    for name, (base, spread) in spreads.items():
        noise = np.random.default_rng([zlib.crc32(name.encode()), seed]).standard_normal(out[name].shape)
        drawn = base * np.exp(spread * noise) if base else spread * noise
        out[name] = jnp.asarray(drawn.astype(out[name].dtype))
    for name, factor in factors.items():
        out[name] = (out[name] * factor).astype(out[name].dtype)
    return out
```

```python
import concourse.bass as bass
from concourse import mybir
from contextlib import ExitStack

N = 128
D = 512
DB = D // 128
E = 4096
EC = E // 128
SB = 4
SBC = EC // SB
HALF = 512
H = 8
DH = D // H
F0 = 4 * D
F0B = F0 // 128
F2 = 2 * D
F2B = F2 // 128
F3 = 64
MUL = 128
RB = 8
HID = 64
EPS = 1e-5
NEG = -1e9
SILU_2MOM = 1.679177
AVG_NEIGH = 10.0
UNROLL = 4

C_BQK, C_BV, C_LN1W, C_LN1B, C_LN2W, C_LN2B = 0, 8, 12, 16, 20, 24
C_B1, C_L2B1, C_EPS, C_Y = 28, 44, 52, 53
C_ALL = C_Y + 4 * EC


def gnn_stack(nc, x_d, cols_d, idx_d, srow_d, feat_d, wm1_d, wm23_d, w4_d, brow_d, b31_d,
              wqk_d, wv_d, wout_d, w1_d, w2_d, wup_d, wo_d, l2w1_d, l2w2_d, l3w1_d, l3w2_d, out_d):
    f32, bf16, f32r, i32 = mybir.dt.float32, mybir.dt.bfloat16, mybir.dt.float32r, mybir.dt.int32
    ALU, ACT, AX = mybir.AluOpType, mybir.ActivationFunctionType, mybir.AxisListType

    ctx = ExitStack()
    with ctx:
        base = (nc.sbuf_base + 63) // 64 * 64
        size = {f32: 4, f32r: 4, i32: 4, bf16: 2}

        def at(name, offset, shape, dt):
            return nc.alloc_sbuf_tensor_at(name, shape, dt, offset=offset)

        cursor = [base]

        def sb(name, shape, dt):
            n = size[dt]
            for s in shape[1:]:
                n *= s
            t = at(name, cursor[0], shape, dt)
            cursor[0] += (n + 63) // 64 * 64
            return t

        o_wqk = cursor[0]
        wqk = sb("wqk", [128, DB, 2 * D], f32)
        l2w1 = at("l2w1", o_wqk, [128, DB, F2], f32)
        o_wv = cursor[0]
        wv = sb("wv", [128, DB, D], f32)
        wout = sb("wout", [128, DB, D], f32)
        l2w2 = at("l2w2", o_wv, [128, F2B, D], f32)
        o_w1 = cursor[0]
        w1 = sb("w1", [128, 4, DB, 512], f32)
        o_w2 = cursor[0]
        w2 = sb("w2", [128, F0B, D], f32)
        wup = sb("wup", [128, 2, MUL], f32)
        wo = sb("wo", [128, 4, MUL], f32)
        wm1 = sb("wm1", [2 * RB, 128], f32)
        wm23 = sb("wm23", [128, 2, 128], f32)
        w4 = sb("w4", [128, 4 * MUL], f32)
        w4hi = sb("w4hi", [128, 4 * MUL], f32r)
        w4lo = sb("w4lo", [128, 4 * MUL], f32r)
        l3w1 = sb("l3w1", [128, DB, F3], f32)
        l3w2 = sb("l3w2", [F3 + 1, D], f32)
        o_tpw = cursor[0]
        tpw = sb("tpw", [128, EC, 4 * MUL], f32)
        chunk_bytes = 4 * MUL * 4
        stk = [at(f"stk{s}", o_tpw + (26 + 2 * s) * chunk_bytes, [128, 2, HALF], f32r) for s in range(3)]
        stk.append(sb("stk3", [128, 2, HALF], f32r))
        qkT = at("qkT", o_tpw + 20 * chunk_bytes, [128, 8, 128], f32)
        prob = at("prob", o_tpw + 22 * chunk_bytes, [128, H, 128], f32)
        probT = at("probT", o_tpw + 24 * chunk_bytes, [128, H, 128], f32)
        hid0T = at("hid0T", o_wqk, [128, F0B, 128], f32)
        feat = at("feat", o_w1, [2 * RB, SB, HALF], f32)
        hid = [at(f"hid{i}", o_w1 + (i + 1) * 4 * SB * HALF, [128, SB, HALF], f32) for i in range(2)]
        ohs = at("ohs", o_w2, [128, EC, 128], bf16)
        ohd = at("ohd", o_w2 + EC * 256, [128, EC, 128], bf16)
        o = o_w1
        gsel = [at(f"gsel{i}", o + i * 512, [128, 128], f32r) for i in range(2)]
        o += 1024
        oh = [at(f"oh{i}", o + i * 512, [128, 128], f32) for i in range(2)]
        o += 1024
        ysel = [at(f"ysel{i}", o + i * 2048, [128, 4, 128], f32) for i in range(2)]
        o += 4096
        prod = [at(f"prod{i}", o + i * 3072, [128, 6, 128], f32) for i in range(2)]
        o += 6144
        tdot = [at(f"tdot{i}", o + i * 512, [128, 128], f32) for i in range(2)]
        o += 1024
        src_i = at("src_i", o, [128, E], i32)
        assert o + 4 * E <= o_w2
        xup_hi = at("xup_hi", o_w2, [128, D], f32r)
        xup_lo = at("xup_lo", o_w2 + 2048, [128, D], f32r)
        msg = at("msg", o_w2 + 4096, [128, 8, 128], f32)
        msgT = at("msgT", o_w2 + 8192, [128, 8, 128], f32)
        hid2T = at("hid2T", o_w2 + 12288, [128, F2B, 128], f32)
        cols = sb("cols", [128, C_ALL], f32)
        idx_i = sb("idx_i", [128, 2, EC], i32)
        idx_b = sb("idx_b", [128, 2, EC], bf16)
        dst_f = sb("dst_f", [128, EC], f32)
        brow = sb("brow", [128, 3, D], f32)
        b31 = sb("b31", [1, F3], f32)
        ones = sb("ones", [1, 128], f32)
        ident = sb("ident", [128, 128], f32)
        iota_row = sb("iota_row", [128, 128], f32)
        iota_rb = sb("iota_rb", [128, 128], bf16)
        iota_p = sb("iota_p", [128, 1], f32)
        neghalf = sb("neghalf", [128, 1], f32)
        eps1 = sb("eps1", [128, 1], f32)
        mask = sb("mask", [128, 128], f32)
        adj = sb("adj", [128, 128], f32)
        cnt_sd = sb("cnt_sd", [128, 128], f32)
        cnt_ds = sb("cnt_ds", [128, 128], f32)
        xs = sb("xs", [128, D], f32)
        hn = sb("hn", [128, D], f32)
        zn = sb("zn", [128, D], f32)
        xr = sb("xr", [128, D], f32)
        un = sb("un", [128, D], f32)
        hT = sb("hT", [128, DB, 128], f32)
        stats = sb("stats", [128, 6], f32)
        mv = sb("mv", [128, 2], f32)
        ve = sb("ve", [128, 1], f32)
        rstd = sb("rstd", [128, 1], f32)
        vn = sb("vn", [128, D], f32)
        smax = sb("smax", [128, H], f32)
        ssum = sb("ssum", [128, H], f32)
        srec = sb("srec", [128, H], f32)
        oT = sb("oT", [128, DB, 128], f32)
        r3 = sb("r3", [128, F3 + 1], f32)
        zT = sb("zT", [F3 + 1, 128], f32)
        assert cursor[0] <= nc.sbuf_usable_end, (cursor[0], nc.sbuf_usable_end)

        P = [ctx.enter_context(nc.psum_tensor(f"bank{i}", [128, 512], f32)) for i in range(8)]

        def sem(name):
            return ctx.enter_context(nc.semaphore(name))

        in_x, in_cols, in_idx, in_srow, in_feat, in_wm = (sem(f"in_{n}") for n in ("x", "cols", "idx", "srow", "feat", "wm"))
        in_w4, in_brow, in_wqk, in_wv, in_wout = (sem(f"in_{n}") for n in ("w4", "brow", "wqk", "wv", "wout"))
        in_small = sem("in_small")
        in_w1 = [sem(f"in_w1_{j}") for j in range(4)]
        in_w2 = [sem(f"in_w2_{j}") for j in range(4)]
        in_l2w1, in_l2w2, out_sent = sem("in_l2w1"), sem("in_l2w2"), sem("out_sent")
        consts_ready, iota_cast, zeroed, idx_cast = (
            sem(n) for n in ("consts_ready", "iota_cast", "zeroed", "idx_cast"))
        var_ready, rstd_ready, dve_chain = sem("var_ready"), sem("rstd_ready"), sem("dve_chain")
        h_ready, hT_ready, hT_act, hT_dve = sem("h_ready"), sem("hT_ready"), sem("hT_act"), sem("hT_dve")
        rad_mm, rad_act, split_ready, w4_split = sem("rad_mm"), sem("rad_act"), sem("split_ready"), sem("w4_split")
        tpw_mm, tpw_act, tpw_dve = sem("tpw_mm"), sem("tpw_act"), sem("tpw_dve")
        onehots, counts_mm, counts_ready = sem("onehots"), sem("counts_mm"), sem("counts_ready")
        qk_mm, v_mm, qk_ready, v_ready = sem("qk_mm"), sem("v_mm"), sem("qk_ready"), sem("v_ready")
        scores_mm, max_ready, exp_ready, prob_ready = sem("scores_mm"), sem("max_ready"), sem("exp_ready"), sem("prob_ready")
        probT_mm, probT_act, probT_dve = sem("probT_mm"), sem("probT_act"), sem("probT_dve")
        o_mm, o_ready, proj_mm, hb_ready, xr_ready = (
            sem("o_mm"), sem("o_ready"), sem("proj_mm"), sem("hb_ready"), sem("xr_ready"))
        up_mm, up_act, up_dve, down_mm, res_ready = sem("up_mm"), sem("up_act"), sem("up_dve"), sem("down_mm"), sem("res_ready")
        lift_mm, lift_hi, lift_ready = sem("lift_mm"), sem("lift_hi"), sem("lift_ready")
        gsel_ready, oh_ready, ysel_ready = sem("gsel_ready"), sem("oh_ready"), sem("ysel_ready")
        gathered, t_steps, prod_ready, scattered = sem("gathered"), sem("t_steps"), sem("prod_ready"), sem("scattered")
        msg_dve, msg_act, msgT_mm, msgT_dve, msgT_act = (
            sem("msg_dve"), sem("msg_act"), sem("msgT_mm"), sem("msgT_dve"), sem("msgT_act"))
        l1_mm, l1_done = sem("l1_mm"), sem("l1_done")
        rst_mm, rst_ready, up2_mm, up2_act, up2_dve, down2_mm, hb2_ready = (
            sem(n) for n in ("rst_mm", "rst_ready", "up2_mm", "up2_act", "up2_dve", "down2_mm", "hb2_ready"))
        r3_mm, r3_ready, z3_mm, z3_ready, out_mm, out_ready = (
            sem(n) for n in ("r3_mm", "r3_ready", "z3_mm", "z3_ready", "out_mm", "out_ready"))

        def y_of(c, m):
            return cols[:, bass.ds(C_Y + 4 * c + m, 1)]

        block = ctx.enter_context(nc.Block())

        @block.sync
        def _(sp):
            sp.dma_start(xs[:, :], x_d).then_inc(in_x, 16)
            sp.dma_start(feat[:, :, :], feat_d).then_inc(in_feat, 16)
            sp.dma_start(wm1[:, :], wm1_d).then_inc(in_wm, 16)
            sp.dma_start(wm23[:, :, :], wm23_d).then_inc(in_wm, 16)
            sp.dma_start(cols[:, :], cols_d).then_inc(in_cols, 16)
            sp.dma_start(idx_i[:, :, :], idx_d).then_inc(in_idx, 16)
            sp.dma_start(w4[:, :], w4_d).then_inc(in_w4, 16)
            sp.dma_start(wqk[:, :, :], wqk_d).then_inc(in_wqk, 16)
            sp.dma_start(wv[:, :, :], wv_d).then_inc(in_wv, 16)
            sp.dma_start(brow[:, :, :], brow_d.partition_broadcast(128)).then_inc(in_brow, 16)
            sp.dma_start(wout[:, :, :], wout_d).then_inc(in_wout, 16)
            sp.dma_start(wup[:, :, :], wup_d).then_inc(in_small, 16)
            sp.dma_start(wo[:, :, :], wo_d).then_inc(in_small, 16)
            sp.dma_start(l3w1[:, :, :], l3w1_d).then_inc(in_small, 16)
            sp.dma_start(l3w2[:, :], l3w2_d).then_inc(in_small, 16)
            sp.dma_start(b31[:, :], b31_d).then_inc(in_small, 16)
            sp.wait_ge(rad_mm, 12)
            sp.wait_ge(split_ready, SB)
            for j in range(4):
                sp.dma_start(w1[:, j, :, :], w1_d[:, j, :, :]).then_inc(in_w1[j], 16)
            sp.wait_ge(counts_mm, 2)
            for j in range(4):
                sp.dma_start(w2[:, 4 * j:4 * j + 4, :], w2_d[:, 4 * j:4 * j + 4, :]).then_inc(in_w2[j], 16)
            sp.wait_ge(up_mm, F0B)
            sp.dma_start(src_i[:, :], srow_d.partition_broadcast(128)).then_inc(in_srow, 16)
            sp.wait_ge(down_mm, 1)
            sp.dma_start(l2w1[:, :, :], l2w1_d).then_inc(in_l2w1, 16)
            sp.wait_ge(proj_mm, 1)
            sp.dma_start(l2w2[:, :, :], l2w2_d).then_inc(in_l2w2, 16)
            sp.wait_ge(out_ready, 1)
            sp.dma_start(out_d, un[:, :]).then_inc(out_sent, 16)
            sp.wait_ge(out_sent, 16)

        @block.gpsimd
        def _(pool):
            pool.memset(neghalf[:, :], -0.5).then_inc(consts_ready, 1)
            pool.iota(iota_row[:, :], pattern=[[1, 128]], base=0, channel_multiplier=0,
                      allow_small_or_imprecise_dtypes=True).then_inc(consts_ready, 1)
            pool.iota(iota_p[:, :], pattern=[[1, 1]], base=0, channel_multiplier=1,
                      allow_small_or_imprecise_dtypes=True).then_inc(consts_ready, 1)
            pool.memset(ones[:, :], 1.0).then_inc(consts_ready, 1)
            pool.memset(ident[:, :], 0.0).then_inc(zeroed, 1)
            pool.wait_ge(zeroed, 1)
            pool.affine_select(out=ident[:, :], in_=ident[:, :], compare_op=ALU.not_equal, fill=1.0,
                               base=0, pattern=[[-1, 128]], channel_multiplier=1).then_inc(consts_ready, 1)

            def root(n):
                pool.wait_ge(var_ready, n)
                pool.tensor_tensor(rstd[:, :], ve[:, :], neghalf[:, :], ALU.pow).then_inc(rstd_ready, 1)

            pool.wait_ge(consts_ready, 5)
            root(1)
            root(2)
            pool.wait_ge(h_ready, 1)
            pool.wait_ge(in_brow, 16)
            pool.tensor_tensor(un[:, :], hn[:, :], brow[:, 0, :], ALU.add).then_inc(hb_ready, 1)
            pool.tensor_tensor(xs[:, :], xs[:, :], brow[:, 1, :], ALU.add).then_inc(hb_ready, 1)
            root(3)
            pool.wait_ge(xr_ready, 1)
            pool.wait_ge(hb_ready, 2)
            pool.tensor_tensor(xs[:, :], xs[:, :], xr[:, :], ALU.add).then_inc(hb_ready, 1)
            root(4)

            pool.wait_ge(up_mm, F0B)
            pool.wait_ge(in_srow, 16)
            pool.wait_ge(idx_cast, 2)
            for c in range(EC):
                b = c % 2
                if c >= 2:
                    pool.wait_ge(gathered, c - 1)
                pool.tensor_scalar(gsel[b][:, :], src_i[:, c * 128:(c + 1) * 128], iota_p[:, :], None,
                                   ALU.is_equal).then_inc(gsel_ready, 1)
                if c >= 2:
                    pool.wait_ge(scattered, c - 1)
                pool.tensor_scalar(oh[b][:, :], iota_row[:, :], dst_f[:, c:c + 1], None,
                                   ALU.is_equal).then_inc(oh_ready, 1)
            root(5)
            pool.wait_ge(h_ready, 5)
            pool.tensor_tensor(un[:, :], hn[:, :], brow[:, 2, :], ALU.add).then_inc(hb2_ready, 1)
            pool.wait_ge(hb2_ready, 1)
            pool.tensor_tensor(xs[:, :], xs[:, :], un[:, :], ALU.add).then_inc(hb2_ready, 1)
            root(6)

        @block.scalar
        def _(act):
            act.preload_act_table(ACT.Silu)

            def radial(layer):
                for s in range(SB):
                    act.wait_ge(rad_mm, SB * layer + s + 1)
                    scale = RB ** -0.5 if layer == 0 else SILU_2MOM * HID ** -0.5
                    act.activation(hid[layer % 2][:, s, :], P[4 + s][:, :], ACT.Silu,
                                   scale=scale).then_inc(rad_act, 1)

            def tpw_out(cs):
                for c in cs:
                    act.wait_ge(tpw_mm, c + 1)
                    act.activation(tpw[:, c, :], P[4 + c % 4][:, :], ACT.Copy,
                                   scale=SILU_2MOM * HID ** -0.5).then_inc(tpw_act, 1)

            radial(0)
            radial(1)
            act.wait_ge(in_cols, 16)
            act.wait_ge(hT_ready, 1)
            for j in (2, 3):
                act.activation(hT[:, j, :], P[1][:, (j - 2) * 128:(j - 1) * 128], ACT.Identity,
                               scale=cols[:, C_LN1W + j:C_LN1W + j + 1],
                               bias=cols[:, C_LN1B + j:C_LN1B + j + 1]).then_inc(hT_act, 1)
            radial(2)
            tpw_out(range(0, 8, 2))
            act.wait_ge(v_mm, 1)
            act.activation(vn[:, :], P[0][:, :], ACT.Copy).then_inc(v_ready, 1)
            for g in range(2):
                act.wait_ge(max_ready, g + 1)
                for b in range(4):
                    s = 4 * g + b
                    act.activation(prob[:, s, :], prob[:, s, :], ACT.Exp, bias=smax[:, s:s + 1],
                                   accum_out=ssum[:, s:s + 1]).then_inc(exp_ready, 1)
            tpw_out(range(8, 16, 2))
            act.wait_ge(probT_mm, 2)
            act.activation(probT[:, 4:8, :], P[1][:, :], ACT.Copy).then_inc(probT_act, 1)
            tpw_out(range(16, 24, 2))
            act.wait_ge(hT_ready, 2)
            for j in (2, 3):
                act.activation(hT[:, j, :], P[1][:, (j - 2) * 128:(j - 1) * 128], ACT.Identity,
                               scale=cols[:, C_LN2W + j:C_LN2W + j + 1],
                               bias=cols[:, C_LN2B + j:C_LN2B + j + 1]).then_inc(hT_act, 1)
            for j in range(1, F0B, 2):
                act.wait_ge(up_mm, j + 1)
                act.activation(hid0T[:, j, :], P[j % 3][:, 0:128], ACT.Relu,
                               bias=cols[:, C_B1 + j:C_B1 + j + 1]).then_inc(up_act, 1)
            tpw_out(range(24, 32, 2))
            act.wait_ge(hT_ready, 3)
            act.activation(hT[:, 2:4, :], P[1][:, 0:256], ACT.Copy).then_inc(hT_act, 1)

            def weigh(c, k, first):
                act.wait_ge(oh_ready, c + 1)
                if not (first and k < 2):
                    act.wait_ge(scattered, c - 1)
                for m in range(4):
                    last = act.activation(ysel[k % 2][:, m, :], oh[k % 2][:, :], ACT.Copy, scale=y_of(c, m))
                last.then_inc(ysel_ready, 1)

            for k in range(UNROLL):
                weigh(k, k, True)
            with act.Fori(1, EC // UNROLL) as i:
                for k in range(UNROLL):
                    weigh(i * UNROLL + k, k, False)
            act.wait_ge(scattered, EC)
            act.activation(msg[:, 4:7, :], P[7][:, 0:384], ACT.Copy).then_inc(msg_act, 1)
            act.activation(msg[:, 7, :], P[7][:, 384:512], ACT.Copy, scale=3.0 ** -0.5).then_inc(msg_act, 1)
            act.wait_ge(msgT_mm, 2)
            act.activation(msgT[:, 4:8, :], P[1][:, :], ACT.Copy).then_inc(msgT_act, 1)
            for j in range(1, F2B, 2):
                act.wait_ge(up2_mm, j + 1)
                act.activation(hid2T[:, j, :], P[(1, 2, 4, 5)[j % 4]][:, 0:128], ACT.Relu,
                               bias=cols[:, C_L2B1 + j:C_L2B1 + j + 1]).then_inc(up2_act, 1)
            act.wait_ge(hT_ready, 4)
            act.activation(hT[:, 2:4, :], P[1][:, 0:256], ACT.Copy).then_inc(hT_act, 1)

        @block.vector
        def _(dve):
            chained = [0]

            def link(ins):
                chained[0] += 1
                ins.then_inc(dve_chain, 1)
                dve.wait_ge(dve_chain, chained[0])

            def stat(src):
                link(dve.bn_stats(stats[:, :], src))
                link(dve.bn_aggr(mv[:, :], stats[:, :]))
                dve.tensor_scalar(ve[:, :], mv[:, 1:2], EPS, None, ALU.add).then_inc(var_ready, 1)

            def relu_norm(n):
                stat(xs[:, :])
                link(dve.tensor_scalar(hn[:, :], xs[:, :], mv[:, 0:1], 0.0, ALU.subtract, ALU.max))
                dve.wait_ge(rstd_ready, n)
                ins = dve.tensor_scalar(hn[:, :], hn[:, :], rstd[:, :], None, ALU.mult)
                ins.then_inc(h_ready, 1)

            def affine_norm(src, n):
                stat(src)
                dve.wait_ge(rstd_ready, n)
                dve.tensor_scalar(zn[:, :], src, mv[:, 0:1], rstd[:, :], ALU.subtract, ALU.mult)\
                   .then_inc(h_ready, 1)

            def tpw_out(cs):
                for c in cs:
                    dve.wait_ge(tpw_mm, c + 1)
                    dve.tensor_scalar(tpw[:, c, :], P[4 + c % 4][:, :], SILU_2MOM * HID ** -0.5, None,
                                      ALU.mult).then_inc(tpw_dve, 1)

            dve.wait_ge(in_x, 16)
            relu_norm(1)
            dve.wait_ge(h_ready, 1)
            affine_norm(hn[:, :], 2)
            dve.wait_ge(consts_ready, 5)
            link(dve.tensor_copy(iota_rb[:, :], iota_row[:, :]))
            dve.wait_ge(in_idx, 16)
            dve.tensor_copy(idx_b[:, :, :], idx_i[:, :, :]).then_inc(idx_cast, 1)
            dve.tensor_copy(dst_f[:, :], idx_i[:, 1, :]).then_inc(idx_cast, 1)
            dve.wait_ge(in_cols, 16)
            dve.wait_ge(hT_ready, 1)
            for j in (0, 1):
                dve.tensor_scalar(hT[:, j, :], P[0][:, j * 128:(j + 1) * 128],
                                  cols[:, C_LN1W + j:C_LN1W + j + 1], cols[:, C_LN1B + j:C_LN1B + j + 1],
                                  ALU.mult, ALU.add).then_inc(hT_dve, 1)
            dve.wait_ge(in_w4, 16)
            link(dve.tensor_copy(w4hi[:, :], w4[:, :]))
            dve.tensor_tensor(w4lo[:, :], w4[:, :], w4hi[:, :], ALU.subtract).then_inc(w4_split, 1)
            for s in range(SB):
                dve.wait_ge(rad_act, 2 * SB + s + 1)
                h = hid[0][:, s, :]
                dve.tensor_copy(stk[s][0:64, 0, :], h[0:64, :]).then_inc(dve_chain, 1)
                link(dve.tensor_copy(stk[s][64:128, 1, :], h[64:128, :]))
                chained[0] += 1
                dve.wait_ge(dve_chain, chained[0])
                link(dve.tensor_tensor(stk[s][64:128, 0, :], h[0:64, :], stk[s][0:64, 0, :], ALU.subtract))
                dve.tensor_tensor(stk[s][0:64, 1, :], h[64:128, :], stk[s][64:128, 1, :], ALU.subtract)\
                   .then_inc(split_ready, 1)
            dve.wait_ge(idx_cast, 2)
            for k, t in ((0, ohs), (1, ohd)):
                dve.tensor_tensor(t[:, :, :], iota_rb[:, :].unsqueeze(1).broadcast_to([128, EC, 128]),
                                  idx_b[:, k, :].unsqueeze(2).broadcast_to([128, EC, 128]),
                                  ALU.is_equal).then_inc(onehots, 1)
            for g in range(2):
                dve.wait_ge(qk_mm, g + 1)
                dve.tensor_tensor(qkT[:, 4 * g:4 * g + 4, :],
                                  P[2 + g][:, :].rearrange("p (b n) -> p b n", b=4),
                                  cols[:, C_BQK + 4 * g:C_BQK + 4 * g + 4].unsqueeze(2).broadcast_to([128, 4, 128]),
                                  ALU.add).then_inc(qk_ready, 1)
            tpw_out(range(1, 8, 2))
            dve.wait_ge(counts_mm, 2)
            link(dve.tensor_tensor(adj[:, :], P[1][:, 0:128], ident[:, :], ALU.add))
            dve.tensor_scalar(eps1[:, :], cols[:, C_EPS:C_EPS + 1], 1.0, None, ALU.add).then_inc(dve_chain, 1)
            link(dve.tensor_scalar(mask[:, :], adj[:, :], 0.5, NEG, ALU.is_lt, ALU.mult))
            chained[0] += 1
            dve.wait_ge(dve_chain, chained[0])
            dve.scalar_tensor_tensor(out=cnt_sd[:, :], in0=ident[:, :], scalar=eps1[:, :], in1=P[1][:, 0:128],
                                     op0=ALU.mult, op1=ALU.add).then_inc(counts_ready, 1)
            dve.tensor_tensor(cnt_ds[:, :], P[1][:, 128:256], ident[:, :], ALU.add).then_inc(counts_ready, 1)
            for g in range(2):
                dve.wait_ge(scores_mm, g + 1)
                link(dve.scalar_tensor_tensor(out=prob[:, 4 * g:4 * g + 4, :],
                                              in0=P[2 + g][:, :].rearrange("p (b n) -> p b n", b=4),
                                              scalar=DH ** -0.5,
                                              in1=mask[:, :].unsqueeze(1).broadcast_to([128, 4, 128]),
                                              op0=ALU.mult, op1=ALU.add))
                link(dve.tensor_reduce(smax[:, 4 * g:4 * g + 4], prob[:, 4 * g:4 * g + 4, :], AX.X, ALU.max))
                dve.tensor_scalar(smax[:, 4 * g:4 * g + 4], smax[:, 4 * g:4 * g + 4], -1.0, None,
                                  ALU.mult).then_inc(max_ready, 1)
            for g in range(2):
                dve.wait_ge(exp_ready, 4 * g + 4)
                link(dve.reciprocal(srec[:, 4 * g:4 * g + 4], ssum[:, 4 * g:4 * g + 4]))
                for b in range(4):
                    s = 4 * g + b
                    dve.tensor_scalar(prob[:, s, :], prob[:, s, :], srec[:, s:s + 1], None,
                                      ALU.mult).then_inc(prob_ready, 1)
                if g == 0:
                    tpw_out(range(9, 16, 2))
            dve.wait_ge(probT_mm, 1)
            dve.tensor_copy(probT[:, 0:4, :], P[0][:, :].rearrange("p (b n) -> p b n", b=4)).then_inc(probT_dve, 1)
            dve.wait_ge(o_mm, 1)
            dve.tensor_tensor(oT[:, :, :], P[2][:, :].rearrange("p (b n) -> p b n", b=4),
                              cols[:, C_BV:C_BV + 4].unsqueeze(2).broadcast_to([128, 4, 128]),
                              ALU.add).then_inc(o_ready, 1)
            tpw_out(range(17, 24, 2))
            dve.wait_ge(proj_mm, 1)
            dve.wait_ge(hb_ready, 1)
            dve.tensor_tensor(xr[:, :], P[3][:, :], un[:, :], ALU.add).then_inc(xr_ready, 1)
            dve.wait_ge(xr_ready, 1)
            affine_norm(xr[:, :], 3)
            dve.wait_ge(hT_ready, 2)
            for j in (0, 1):
                dve.tensor_scalar(hT[:, j, :], P[0][:, j * 128:(j + 1) * 128],
                                  cols[:, C_LN2W + j:C_LN2W + j + 1], cols[:, C_LN2B + j:C_LN2B + j + 1],
                                  ALU.mult, ALU.add).then_inc(hT_dve, 1)
            for j in range(0, F0B, 2):
                dve.wait_ge(up_mm, j + 1)
                dve.tensor_scalar(hid0T[:, j, :], P[j % 3][:, 0:128], cols[:, C_B1 + j:C_B1 + j + 1], 0.0,
                                  ALU.add, ALU.max).then_inc(up_dve, 1)
            tpw_out(range(25, 32, 2))
            dve.wait_ge(down_mm, 1)
            dve.wait_ge(hb_ready, 3)
            dve.tensor_tensor(xs[:, :], P[3][:, :], xs[:, :], ALU.add).then_inc(res_ready, 1)

            dve.wait_ge(res_ready, 1)
            relu_norm(4)
            dve.wait_ge(hT_ready, 3)
            dve.tensor_copy(hT[:, 0:2, :], P[0][:, 0:256].rearrange("p (b n) -> p b n", b=2)).then_inc(hT_dve, 1)
            dve.wait_ge(lift_mm, 1)
            link(dve.tensor_scalar(xup_hi[:, :], P[4][:, :], MUL ** -0.5, None, ALU.mult))
            dve.scalar_tensor_tensor(out=xup_lo[:, :], in0=P[4][:, :], scalar=MUL ** -0.5, in1=xup_hi[:, :],
                                     op0=ALU.mult, op1=ALU.subtract).then_inc(lift_ready, 1)

            def messages(c, k, first):
                b = k % 2
                g, p, t = P[k], prod[b], tdot[b]
                w = tpw[:, bass.ds(c, 1), :].rearrange("p a (q u) -> p (a q) u", q=4)
                dve.wait_ge(gathered, c + 1)
                if not (first and k < 2):
                    dve.wait_ge(scattered, c - 1)
                dve.tensor_scalar(t[:, :], g[:, 128:256], y_of(c, 1), None, ALU.mult).then_inc(t_steps, 1)
                dve.tensor_tensor(p[:, 0:5:4, :], g[:, 0:128].unsqueeze(1).broadcast_to([128, 2, 128]),
                                  w[:, 0:2, :], ALU.mult)
                dve.wait_ge(t_steps, 3 * c + 1)
                dve.scalar_tensor_tensor(out=t[:, :], in0=g[:, 256:384], scalar=y_of(c, 2), in1=t[:, :],
                                         op0=ALU.mult, op1=ALU.add).then_inc(t_steps, 1)
                dve.wait_ge(t_steps, 3 * c + 2)
                dve.scalar_tensor_tensor(out=t[:, :], in0=g[:, 384:512], scalar=y_of(c, 3), in1=t[:, :],
                                         op0=ALU.mult, op1=ALU.add).then_inc(t_steps, 1)
                dve.tensor_tensor(p[:, 1:4, :], g[:, 128:512].rearrange("p (m u) -> p m u", m=3),
                                  w[:, 2:3, :].broadcast_to([128, 3, 128]), ALU.mult)
                dve.wait_ge(t_steps, 3 * c + 3)
                dve.tensor_tensor(p[:, 5, :], t[:, :], w[:, 3, :], ALU.mult).then_inc(prod_ready, 1)

            for k in range(UNROLL):
                messages(k, k, True)
            with dve.Fori(1, EC // UNROLL) as i:
                for k in range(UNROLL):
                    messages(i * UNROLL + k, k, False)
            dve.wait_ge(scattered, EC)
            dve.tensor_copy(msg[:, 0:4, :], P[6][:, :].rearrange("p (b n) -> p b n", b=4)).then_inc(msg_dve, 1)
            dve.wait_ge(msgT_mm, 1)
            dve.tensor_copy(msgT[:, 0:4, :], P[0][:, :].rearrange("p (b n) -> p b n", b=4)).then_inc(msgT_dve, 1)
            dve.wait_ge(l1_mm, 1)
            final = (2 * MUL) ** -0.5 / AVG_NEIGH
            dve.scalar_tensor_tensor(out=xs[:, 0:128], in0=P[4][:, 0:128], scalar=final, in1=xs[:, 0:128],
                                     op0=ALU.mult, op1=ALU.add).then_inc(l1_done, 1)
            xv = xs[:, 128:512].rearrange("p (v m) -> p m v", m=3)
            dve.scalar_tensor_tensor(out=xv, in0=P[4][:, 128:512].rearrange("p (m v) -> p m v", m=3),
                                     scalar=final, in1=xv, op0=ALU.mult, op1=ALU.add).then_inc(l1_done, 1)

            dve.wait_ge(l1_done, 2)
            relu_norm(5)
            dve.wait_ge(rst_mm, 1)
            dve.tensor_copy(hT[:, :, :], P[0][:, :].rearrange("p (b n) -> p b n", b=4)).then_inc(rst_ready, 1)
            for j in range(0, F2B, 2):
                dve.wait_ge(up2_mm, j + 1)
                dve.tensor_scalar(hid2T[:, j, :], P[(1, 2, 4, 5)[j % 4]][:, 0:128], cols[:, C_L2B1 + j:C_L2B1 + j + 1], 0.0,
                                  ALU.add, ALU.max).then_inc(up2_dve, 1)
            dve.wait_ge(down2_mm, 1)
            dve.wait_ge(hb2_ready, 2)
            dve.tensor_tensor(xs[:, :], P[3][:, :], xs[:, :], ALU.add).then_inc(res_ready, 1)

            dve.wait_ge(res_ready, 2)
            relu_norm(6)
            dve.memset(r3[:, F3:F3 + 1], 1.0).then_inc(r3_ready, 1)
            dve.wait_ge(hT_ready, 4)
            dve.tensor_copy(hT[:, 0:2, :], P[0][:, 0:256].rearrange("p (b n) -> p b n", b=2)).then_inc(hT_dve, 1)
            dve.wait_ge(r3_mm, 1)
            dve.tensor_scalar(r3[:, 0:F3], P[2][:, 0:F3], 0.0, None, ALU.max).then_inc(r3_ready, 1)
            dve.wait_ge(z3_mm, 1)
            dve.tensor_copy(zT[:, :], P[4][0:F3 + 1, 0:128]).then_inc(z3_ready, 1)
            dve.wait_ge(out_mm, 1)
            dve.tensor_tensor(un[:, :], P[5][:, :], xs[:, :], ALU.add).then_inc(out_ready, 1)

        @block.tensor
        def _(pe):
            def transposes(src, n, dsts, signal):
                for j in range(n):
                    last = pe.transpose(dsts[j], src[j], ident[:, :])
                last.then_inc(signal, 1)

            def radial(layer):
                for s in range(SB):
                    if layer == 0:
                        pe.matmul(P[4 + s][:, :], wm1[:, :], feat[:, s, :], start=True, stop=True).then_inc(rad_mm, 1)
                    else:
                        pe.wait_ge(rad_act, SB * (layer - 1) + s + 1)
                        pe.matmul(P[4 + s][:, :], wm23[:, layer - 1, :], hid[(layer - 1) % 2][:, s, :],
                                  start=True, stop=True).then_inc(rad_mm, 1)

            def paths(cs):
                for c in cs:
                    s, half, col = c // SBC, c % SBC // 4, c % 4 * 128
                    if c >= 5 and c % 2 == 0 or c == 4:
                        pe.wait_ge(tpw_act, (c - 4) // 2 + 1)
                    elif c >= 4:
                        pe.wait_ge(tpw_dve, (c - 5) // 2 + 1)
                    h = stk[s][:, half, col:col + 128]
                    pe.matmul(P[4 + c % 4][:, :], h, w4hi[:, :], start=True, stop=False)
                    pe.matmul(P[4 + c % 4][:, :], h, w4lo[:, :], start=False, stop=True).then_inc(tpw_mm, 1)

            def blocks(src):
                return [src[:, j * 128:(j + 1) * 128] for j in range(4)]

            two_banks = [P[j // 2][:, (j % 2) * 128:(j % 2 + 1) * 128] for j in range(4)]

            pe.wait_ge(in_feat, 16)
            pe.wait_ge(in_wm, 32)
            radial(0)
            radial(1)
            pe.wait_ge(consts_ready, 5)
            pe.wait_ge(h_ready, 2)
            transposes(blocks(zn), 4, two_banks, hT_ready)
            radial(2)
            pe.wait_ge(in_wqk, 16)
            pe.wait_ge(hT_act, 2)
            pe.wait_ge(hT_dve, 2)
            for b in range(8):
                for j in range(DB):
                    last = pe.matmul(P[2 + b // 4][:, b % 4 * 128:(b % 4 + 1) * 128], wqk[:, j, b * 128:(b + 1) * 128],
                                     hT[:, j, :], start=j == 0, stop=j == DB - 1)
                if b % 4 == 3:
                    last.then_inc(qk_mm, 1)
            pe.wait_ge(in_wv, 16)
            for j in range(DB):
                last = pe.matmul(P[0][:, :], hT[:, j, :], wv[:, j, :], start=j == 0, stop=j == DB - 1)
            last.then_inc(v_mm, 1)
            pe.wait_ge(w4_split, 1)
            pe.wait_ge(split_ready, SB)
            paths(range(0, 8))
            pe.wait_ge(onehots, 2)
            for g, (a, b) in enumerate(((ohs, ohd), (ohd, ohs))):
                for c in range(EC):
                    last = pe.matmul(P[1][:, g * 128:(g + 1) * 128], a[:, c, :], b[:, c, :],
                                     start=c == 0, stop=c == EC - 1)
                last.then_inc(counts_mm, 1)
            pe.wait_ge(qk_ready, 2)
            for g in range(2):
                rows = slice(64 * g, 64 * g + 64)
                for b in range(4):
                    last = pe.matmul(P[2 + g][:, b * 128:(b + 1) * 128], qkT[rows, b, :], qkT[rows, 4 + b, :],
                                     start=True, stop=True)
                last.then_inc(scores_mm, 1)
            paths(range(8, 16))
            pe.wait_ge(v_ready, 1)
            pe.wait_ge(counts_ready, 2)
            for g in range(2):
                for b in range(4):
                    pe.wait_ge(prob_ready, 4 * g + b + 1)
                    last = pe.transpose(P[g][:, b * 128:(b + 1) * 128], prob[:, 4 * g + b, :], ident[:, :])
                last.then_inc(probT_mm, 1)
            for g in range(2):
                if g == 0:
                    pe.wait_ge(probT_dve, 1)
                else:
                    pe.wait_ge(probT_act, 1)
                for b in range(4):
                    h = 2 * b + g
                    last = pe.matmul(P[2][64 * g:64 * g + 64, b * 128:(b + 1) * 128], vn[:, h * DH:(h + 1) * DH],
                                     probT[:, 4 * g + b, :], start=True, stop=True)
            last.then_inc(o_mm, 1)
            paths(range(16, 20))
            pe.wait_ge(o_ready, 1)
            pe.wait_ge(in_wout, 16)
            for j in range(DB):
                last = pe.matmul(P[3][:, :], oT[:, j, :], wout[:, j, :], start=j == 0, stop=j == DB - 1)
            last.then_inc(proj_mm, 1)
            paths(range(20, 24))
            pe.wait_ge(h_ready, 3)
            transposes(blocks(zn), 4, two_banks, hT_ready)
            pe.wait_ge(hT_act, 4)
            pe.wait_ge(hT_dve, 4)

            def down(j):
                if j % 4 == 0:
                    pe.wait_ge(in_w2[j // 4], 16)
                if j % 2:
                    pe.wait_ge(up_act, j // 2 + 1)
                else:
                    pe.wait_ge(up_dve, j // 2 + 1)
                return pe.matmul(P[3][:, :], hid0T[:, j, :], w2[:, j, :], start=j == 0, stop=j == F0B - 1)

            for f in range(F0B):
                if f % 4 == 0:
                    pe.wait_ge(in_w1[f // 4], 16)
                for j in range(DB):
                    last = pe.matmul(P[f % 3][:, 0:128], w1[:, f // 4, j, f % 4 * 128:(f % 4 + 1) * 128],
                                     hT[:, j, :], start=j == 0, stop=j == DB - 1, skip_group_check=True)
                last.then_inc(up_mm, 1)
                if f >= 2:
                    down(f - 2)
            down(F0B - 2)
            down(F0B - 1).then_inc(down_mm, 1)
            paths(range(24, 32))

            pe.wait_ge(in_small, 80)
            pe.wait_ge(h_ready, 4)
            views = [hn[:, 0:128]] + [hn[:, 128 + m:512:3] for m in range(3)]
            transposes(views, 4, two_banks, hT_ready)
            pe.wait_ge(hT_act, 5)
            pe.wait_ge(hT_dve, 5)
            pe.wait_ge(tpw_act, 15)
            for j in range(4):
                last = pe.matmul(P[4][:, j * 128:(j + 1) * 128], hT[:, j, :], wup[:, min(j, 1), :], start=True, stop=True)
            last.then_inc(lift_mm, 1)
            pe.wait_ge(lift_ready, 1)
            pe.wait_ge(tpw_act, 16)
            pe.wait_ge(tpw_dve, 16)

            def gather(c, k, first):
                pe.wait_ge(gsel_ready, c + 1)
                if not first:
                    pe.wait_ge(prod_ready, c - UNROLL + 1)
                pe.matmul(P[k][:, :], gsel[k % 2][:, :], xup_hi[:, :], start=True, stop=False)
                pe.matmul(P[k][:, :], gsel[k % 2][:, :], xup_lo[:, :], start=False, stop=True).then_inc(gathered, 1)

            def scatter(c, k, first, last):
                p, y = prod[k % 2], ysel[k % 2]
                pe.wait_ge(ysel_ready, c + 1)
                pe.wait_ge(prod_ready, c + 1)
                pe.matmul(P[6][:, :], y[:, 0, :], p[:, 0:4, :], start=first, stop=last, skip_group_check=True)
                for m in range(3):
                    pe.matmul(P[7][:, m * 128:(m + 1) * 128], y[:, m + 1, :], p[:, 4, :],
                              start=first and m == 0, stop=last, skip_group_check=True)
                pe.matmul(P[7][:, 384:512], oh[k % 2][:, :], p[:, 5, :], start=False, stop=last,
                          skip_group_check=True).then_inc(scattered, 1)

            for k in range(UNROLL):
                gather(k, k, True)
                if k >= 1:
                    scatter(k - 1, k - 1, k == 1, False)
            with pe.Fori(1, EC // UNROLL) as i:
                for k in range(UNROLL):
                    gather(i * UNROLL + k, k, False)
                    scatter(i * UNROLL + (k - 1), (k - 1) % UNROLL, False, False)
            scatter(EC - 1, UNROLL - 1, False, True)
            pe.wait_ge(msg_dve, 1)
            for j in range(4):
                last = pe.transpose(P[0][:, j * 128:(j + 1) * 128], msg[:, j, :], ident[:, :])
            last.then_inc(msgT_mm, 1)
            pe.wait_ge(msg_act, 2)
            for j in range(4):
                last = pe.transpose(P[1][:, j * 128:(j + 1) * 128], msg[:, 4 + j, :], ident[:, :])
            last.then_inc(msgT_mm, 1)
            pe.wait_ge(msgT_dve, 1)
            pe.wait_ge(msgT_act, 1)
            for n, (j, ja) in enumerate(((0, 7), (4, 1), (5, 2), (6, 3))):
                g = 0 if n == 0 else 2
                pe.matmul(P[4][:, n * 128:(n + 1) * 128], msgT[:, j, :], wo[:, g, :], start=True, stop=False)
                last = pe.matmul(P[4][:, n * 128:(n + 1) * 128], msgT[:, ja, :], wo[:, g + 1, :], start=False, stop=True)
            last.then_inc(l1_mm, 1)

            pe.wait_ge(h_ready, 5)
            for j in range(DB):
                last = pe.matmul(P[0][:, j * 128:(j + 1) * 128], hn[:, j * 128:(j + 1) * 128], cnt_sd[:, :],
                                 start=True, stop=True)
            last.then_inc(rst_mm, 1)
            pe.wait_ge(rst_ready, 1)
            pe.wait_ge(in_l2w1, 16)
            pe.wait_ge(in_l2w2, 16)
            pe.wait_ge(l1_done, 2)

            def down2(j):
                if j % 2:
                    pe.wait_ge(up2_act, j // 2 + 1)
                else:
                    pe.wait_ge(up2_dve, j // 2 + 1)
                return pe.matmul(P[3][:, :], hid2T[:, j, :], l2w2[:, j, :], start=j == 0, stop=j == F2B - 1)

            for f in range(F2B):
                for j in range(DB):
                    last = pe.matmul(P[(1, 2, 4, 5)[f % 4]][:, 0:128], l2w1[:, j, f * 128:(f + 1) * 128], hT[:, j, :],
                                     start=j == 0, stop=j == DB - 1, skip_group_check=True)
                last.then_inc(up2_mm, 1)
                if f >= 2:
                    down2(f - 2)
            down2(F2B - 2)
            down2(F2B - 1).then_inc(down2_mm, 1)

            pe.wait_ge(h_ready, 6)
            transposes(blocks(hn), 4, two_banks, hT_ready)
            pe.matmul(P[2][:, 0:F3], ones[:, :], b31[:, :], start=True, stop=False)
            pe.wait_ge(hT_dve, 6)
            pe.wait_ge(hT_act, 6)
            for j in range(DB):
                last = pe.matmul(P[2][:, 0:F3], hT[:, j, :], l3w1[:, j, :], start=False, stop=j == DB - 1)
            last.then_inc(r3_mm, 1)
            pe.wait_ge(r3_ready, 2)
            pe.matmul(P[4][0:F3 + 1, 0:128], r3[:, :], cnt_ds[:, :], start=True, stop=True).then_inc(z3_mm, 1)
            pe.wait_ge(z3_ready, 1)
            pe.matmul(P[5][:, :], zT[:, :], l3w2[:, :], start=True, stop=True).then_inc(out_mm, 1)


def kernel(**inputs):
    import numpy as np
    import concourse.bacc as bacc
    from concourse import mybir as _mybir
    from concourse.bass_utils import run_bass_kernel_spmd

    a = {k: np.asarray(v) for k, v in inputs.items()}

    def per_partition(v):
        return v.reshape(-1, 128).T

    def k_major(w):
        return w.reshape(-1, 128, w.shape[1]).transpose(1, 0, 2)

    def twice(w):
        r, c = w.shape
        t = np.zeros((2 * r, 2 * c), w.dtype)
        t[:r, :c] = w
        t[r:, c:] = w
        return t

    b_in = a['L0_gnn_b_in']
    w_in = a['L0_gnn_w_in']
    src, dst = a['src'].astype(np.int32), a['dst'].astype(np.int32)
    y = a['edge_attr_4'].reshape(EC, 128, 4).transpose(1, 0, 2).reshape(128, 4 * EC)
    w2b = np.concatenate([a['L3_gnn_W2'], a['L3_gnn_b2'][None]], 0)
    arrays = {
        'x': a['x'],
        'cols': np.concatenate([per_partition(b_in[:2 * D]), per_partition(b_in[2 * D:]),
                                per_partition(a['L0_gnn_ln1_w']), per_partition(a['L0_gnn_ln1_b']),
                                per_partition(a['L0_gnn_ln2_w']), per_partition(a['L0_gnn_ln2_b']),
                                per_partition(a['L0_gnn_b1']), per_partition(a['L2_gnn_b1']),
                                np.broadcast_to(a['L2_gnn_eps'], (128, 1)), y], 1),
        'idx': np.stack([src.reshape(EC, 128).T, dst.reshape(EC, 128).T], 1),
        'srow': src,
        'feat': a['edge_attr_8'].reshape(SB, 2, HALF, RB).transpose(1, 3, 0, 2).reshape(2 * RB, SB, HALF),
        'wm1': twice(a['L1_gnn_W_mlp1']),
        'wm23': np.stack([twice(a['L1_gnn_W_mlp2']), twice(a['L1_gnn_W_mlp3'])], 1),
        'w4': np.concatenate([a['L1_gnn_W_mlp4']] * 2, 0),
        'brow': np.concatenate([a['L0_gnn_b_out'], a['L0_gnn_b2'], a['L2_gnn_b2']]),
        'b31': a['L3_gnn_b1'][None],
        'wqk': k_major(w_in[:2 * D].T),
        'wv': k_major(w_in[2 * D:].T),
        'wout': k_major(a['L0_gnn_w_out'].T),
        'w1': k_major(a['L0_gnn_w1'].T).reshape(128, DB, 4, 512).transpose(0, 2, 1, 3),
        'w2': k_major(a['L0_gnn_w2'].T),
        'wup': np.stack([a['L1_gnn_W_up0'], a['L1_gnn_W_up1']], 1),
        'wo': np.concatenate([k_major(a['L1_gnn_W_out0']), k_major(a['L1_gnn_W_out1'])], 1),
        'l2w1': k_major(a['L2_gnn_W1']),
        'l2w2': k_major(a['L2_gnn_W2']),
        'l3w1': k_major(a['L3_gnn_W1']),
        'l3w2': w2b,
    }
    arrays = {f"in_{k}": np.ascontiguousarray(v) for k, v in arrays.items()}
    nc = bacc.Bacc("TRN2", target_bir_lowering=False, num_devices=1)
    args = [nc.dram_tensor(k, v.shape, _mybir.dt.from_np(v.dtype), kind="ExternalInput").ap() for k, v in arrays.items()]
    out = nc.dram_tensor("out", (N, D), _mybir.dt.float32, kind="ExternalOutput").ap()
    gnn_stack(nc, *args, out)
    r = run_bass_kernel_spmd(nc, [arrays], core_ids=[0])
    return r.results[0]["out"]
```

```python
import concourse.bass as bass
from concourse import mybir
from contextlib import ExitStack

N = 128
D = 512
DB = D // 128
E = 4096
EC = E // 128
SB = 4
SBC = EC // SB
HALF = 512
H = 8
DH = D // H
F0 = 4 * D
F0B = F0 // 128
F2 = 2 * D
F2B = F2 // 128
F3 = 64
MUL = 128
RB = 8
HID = 64
EPS = 1e-5
NEG = -1e9
SILU_2MOM = 1.679177
AVG_NEIGH = 10.0
T_V, T_SOFT, T_ATTN, T_PROJ, T_NORM2, T_MLP, T_NORM3, T_LIFT = 4, 8, 9, 11, 19, 21, 26, 28
POOL_OH = 10
Y0_POOL = 5
WARM = 12
UNROLL = 4
PATH_SCALE = SILU_2MOM * HID ** -0.5
LAG = 3

C_BQK, C_BV, C_LN1W, C_LN1B, C_LN2W, C_LN2B = 0, 8, 12, 16, 20, 24
C_B1, C_L2B1, C_EPS, C_Y = 28, 44, 52, 53
C_ALL = C_Y + 4 * EC


def gnn_stack(nc, x_d, cols_d, idx_d, srow_d, feat_d, wm23_d, w4_d, brow_d, b31_d,
              wqk_d, wv_d, wout_d, w1_d, w2_d, wup_d, wo_d, l2w1_d, l2w2_d, l3w1_d, l3w2_d, out_d):
    f32, bf16, f32r, i32 = mybir.dt.float32, mybir.dt.bfloat16, mybir.dt.float32r, mybir.dt.int32
    ALU, ACT, AX = mybir.AluOpType, mybir.ActivationFunctionType, mybir.AxisListType

    ctx = ExitStack()
    with ctx:
        base = (nc.sbuf_base + 63) // 64 * 64
        size = {f32: 4, f32r: 4, i32: 4, bf16: 2}

        def at(name, offset, shape, dt):
            return nc.alloc_sbuf_tensor_at(name, shape, dt, offset=offset)

        cursor = [base]

        def sb(name, shape, dt):
            n = size[dt]
            for s in shape[1:]:
                n *= s
            t = at(name, cursor[0], shape, dt)
            cursor[0] += (n + 63) // 64 * 64
            return t

        o_wqk = cursor[0]
        wqk = sb("wqk", [128, DB, 2 * D], f32)
        l2w1 = at("l2w1", o_wqk, [128, DB, F2], f32)
        o_wv = cursor[0]
        wv = sb("wv", [128, DB, D], f32)
        wout = sb("wout", [128, DB, D], f32)
        oh = at("oh", o_wv, [128, EC, 128], f32r)
        o_w1 = cursor[0]
        w1 = sb("w1", [128, 4, DB, 512], f32)
        o_w2 = cursor[0]
        w2 = sb("w2", [128, F0B, D], f32)
        wup = sb("wup", [128, 2, MUL], f32)
        wo = sb("wo", [128, 4, MUL], f32)
        wm23 = sb("wm23", [128, 2, 128], f32)
        w4 = sb("w4", [128, 4 * MUL], f32)
        w4hi = sb("w4hi", [128, 4 * MUL], f32r)
        w4lo = sb("w4lo", [128, 4 * MUL], f32r)
        l3w1 = sb("l3w1", [128, DB, F3], f32)
        l3w2 = sb("l3w2", [F3 + 1, D], f32)
        o_tpw = cursor[0]
        tpw = sb("tpw", [128, EC, 4 * MUL], f32)
        chunk_bytes = 4 * MUL * 4
        stk = [at(f"stk{s}", o_tpw + (26 + 2 * s) * chunk_bytes, [128, 2, HALF], f32r) for s in range(3)]
        stk.append(sb("stk3", [128, 2, HALF], f32r))
        qkT = at("qkT", o_tpw + 20 * chunk_bytes, [128, 8, 128], f32)
        prob = at("prob", o_tpw + 22 * chunk_bytes, [128, H, 128], f32)
        probT = at("probT", o_tpw + 24 * chunk_bytes, [128, H, 128], f32)
        l2w2 = at("l2w2", o_tpw, [128, F2B, D], f32)
        assert F2B == 8
        msg = at("msg", o_tpw + 8 * chunk_bytes, [128, 8, 128], f32)
        msgT = at("msgT", o_tpw + 10 * chunk_bytes, [128, 8, 128], f32)
        hid2T = at("hid2T", o_tpw + 12 * chunk_bytes, [128, F2B, 128], f32)
        hid0T = at("hid0T", o_wqk, [128, F0B, 128], f32)
        assert 4 * 128 * (F0B + EC // 2) <= 4 * DB * 2 * D
        o_src = (o_wqk + 4 * 128 * F0B, o_w1)
        src_i = [at(f"src_i{g}", o_src[g], [128, E // 2], i32) for g in range(2)]
        gsel = [at(f"gsel{g}", o_src[g], [128, EC // 2, 128], f32r) for g in range(2)]
        feat_wm1 = at("feat_wm1", o_w1, [2 * RB, SB * HALF + 128], f32)
        hid = [at(f"hid{i}", o_w1 + 4 * (SB * HALF + 128) + i * 4 * SB * HALF, [128, SB, HALF], f32) for i in range(2)]
        ohs = at("ohs", o_w2, [128, EC, 128], bf16)
        ohd = at("ohd", o_w2 + EC * 256, [128, EC, 128], bf16)
        o = o_w1 + 4 * 128 * (EC // 2)
        ysel = [at(f"ysel{i}", o + i * 1536, [128, 3, 128], f32) for i in range(UNROLL)]
        o += UNROLL * 1536
        tdot = [at(f"tdot{i}", o + i * 512, [128, 128], f32) for i in range(UNROLL)]
        o += UNROLL * 512
        assert o <= o_w2
        xup_hi = at("xup_hi", o_w2, [128, D], f32r)
        xup_lo = at("xup_lo", o_w2 + 2048, [128, D], f32r)
        o = o_w2 + 4096
        prod = [at(f"prod{i}", o + i * 3072, [128, 6, 128], f32) for i in range(UNROLL)]
        o += UNROLL * 3072
        ac_hi = [at(f"ac_hi{i}", o + i * 2048, [128, 512], f32r) for i in range(UNROLL)]
        o += UNROLL * 2048
        ac_lo = [at(f"ac_lo{i}", o + i * 2048, [128, 512], f32r) for i in range(UNROLL)]
        o += UNROLL * 2048
        assert o <= o_w2 + 4 * F0B * D
        warm = sb("warm", [128, D], bf16)
        cols = sb("cols", [128, C_ALL], f32)
        idx_i = sb("idx_i", [128, 2, EC], i32)
        end_f = sb("end_f", [128, 2, EC], f32)
        brow = sb("brow", [128, 3, D], f32)
        b31 = sb("b31", [128, F3], f32)
        ident = sb("ident", [128, 128], f32)
        iota_row = sb("iota_row", [128, 128], f32)
        iota_rb = sb("iota_rb", [128, 128], bf16)
        iota_p = sb("iota_p", [128, 1], f32)
        neghalf = sb("neghalf", [128, 1], f32)
        nscale = sb("nscale", [128, 1], f32)
        cnt_n = sb("cnt_n", [128, 128], f32)
        eps1 = sb("eps1", [128, 1], f32)
        mask = sb("mask", [128, 128], f32)
        adj = sb("adj", [128, 128], f32)
        cnt_sd = sb("cnt_sd", [128, 128], f32)
        cnt_ds = sb("cnt_ds", [128, 128], f32)
        xs = sb("xs", [128, D], f32)
        hn = sb("hn", [128, D], f32)
        zn = sb("zn", [128, D], f32)
        xr = sb("xr", [128, D], f32)
        un = sb("un", [128, D], f32)
        hT = sb("hT", [128, DB, 128], f32)
        y0s = sb("y0s", [128, EC], f32)
        stats = sb("stats", [128, 4, 6], f32)
        mv = sb("mv", [128, 2], f32)
        ve = sb("ve", [128, 1], f32)
        rstd = sb("rstd", [128, 1], f32)
        vn = sb("vn", [128, D], f32)
        smax = sb("smax", [128, H], f32)
        ssum = sb("ssum", [128, H], f32)
        srec = sb("srec", [128, H], f32)
        oT = sb("oT", [128, DB, 128], f32)
        r3 = sb("r3", [128, F3 + 1], f32)
        zT = sb("zT", [F3 + 1, 128], f32)
        assert cursor[0] <= nc.sbuf_usable_end, (cursor[0], nc.sbuf_usable_end)

        P = [ctx.enter_context(nc.psum_tensor(f"bank{i}", [128, 512], f32)) for i in range(8)]

        def sem(name):
            return ctx.enter_context(nc.semaphore(name))

        in_x, in_cols, in_idx, in_feat, in_wm = (sem(f"in_{n}") for n in ("x", "cols", "idx", "feat", "wm"))
        in_srow = [sem(f"in_srow_{g}") for g in range(2)]
        in_w4, in_brow, in_wqk, in_wv, in_wout = (sem(f"in_{n}") for n in ("w4", "brow", "wqk", "wv", "wout"))
        in_small = sem("in_small")
        in_w1 = [sem(f"in_w1_{j}") for j in range(4)]
        in_w2 = [sem(f"in_w2_{j}") for j in range(4)]
        in_l2w1, in_l2w2, out_sent = sem("in_l2w1"), sem("in_l2w2"), sem("out_sent")
        consts_ready, iota_cast, zeroed, idx_cast = (
            sem(n) for n in ("consts_ready", "iota_cast", "zeroed", "idx_cast"))
        warm_ready = sem("warm_ready")
        var_ready, rstd_ready, dve_chain = sem("var_ready"), sem("rstd_ready"), sem("dve_chain")
        h_ready, hT_ready, hT_act, hT_dve = sem("h_ready"), sem("hT_ready"), sem("hT_act"), sem("hT_dve")
        rad_mm, rad_act, split_ready, w4_split = sem("rad_mm"), sem("rad_act"), sem("split_ready"), sem("w4_split")
        hi_ready, tpw_mm, tpw_act, tpw_dve = sem("hi_ready"), sem("tpw_mm"), sem("tpw_act"), sem("tpw_dve")
        onehots_pool = sem("onehots_pool")
        onehots, counts_mm, counts_ready = sem("onehots"), sem("counts_mm"), sem("counts_ready")
        adjT_mm, adjT_ready = sem("adjT_mm"), sem("adjT_ready")
        qk_mm, v_mm, qk_ready, v_ready = sem("qk_mm"), sem("v_mm"), sem("qk_ready"), sem("v_ready")
        scores_mm, max_ready, exp_ready, prob_ready = sem("scores_mm"), sem("max_ready"), sem("exp_ready"), sem("prob_ready")
        probT_mm, probT_act, probT_dve = sem("probT_mm"), sem("probT_act"), sem("probT_dve")
        o_mm, o_ready, proj_mm, hb_ready, xr_ready = (
            sem("o_mm"), sem("o_ready"), sem("proj_mm"), sem("hb_ready"), sem("xr_ready"))
        up_mm, up_act, up_dve, down_mm, res_ready = sem("up_mm"), sem("up_act"), sem("up_dve"), sem("down_mm"), sem("res_ready")
        lift_mm, lift_hi, lift_ready = sem("lift_mm"), sem("lift_hi"), sem("lift_ready")
        gsel_ready, oh_ready, ysel_ready = sem("gsel_ready"), sem("oh_ready"), sem("ysel_ready")
        y0s_ready, y0_in, y0_pool = sem("y0s_ready"), sem("y0_in"), sem("y0_pool")
        t0_ready, ac_ready, ac_rounded, ac_left = sem("t0_ready"), sem("ac_ready"), sem("ac_rounded"), sem("ac_left")
        gathered, t_steps, prod_ready, scattered = sem("gathered"), sem("t_steps"), sem("prod_ready"), sem("scattered")
        msg_dve, msg_act, msgT_mm, msgT_dve, msgT_act = (
            sem("msg_dve"), sem("msg_act"), sem("msgT_mm"), sem("msgT_dve"), sem("msgT_act"))
        bd_done, l1_mm, l1_done = sem("bd_done"), sem("l1_mm"), sem("l1_done")
        rst_mm, rst_ready, up2_mm, up2_act, up2_dve, down2_mm, hb2_ready = (
            sem(n) for n in ("rst_mm", "rst_ready", "up2_mm", "up2_act", "up2_dve", "down2_mm", "hb2_ready"))
        r3_mm, r3_ready, z3_mm, z3_ready, out_mm, out_ready = (
            sem(n) for n in ("r3_mm", "r3_ready", "z3_mm", "z3_ready", "out_mm", "out_ready"))

        by_dve = (1, 2, 26)

        def taken(c):
            n = sum(1 for k in by_dve if k <= c)
            return (tpw_dve, n) if c in by_dve else (tpw_act, c + 1 - n)

        def path_views(c):
            return (tpw[:, c, :].rearrange("p (q u) -> p q u", q=4), P[4 + c % 4][:, :].rearrange("p (q u) -> p q u", q=4))

        def y_of(c, m):
            return cols[:, bass.ds(C_Y + 4 * c + m, 1)]

        block = ctx.enter_context(nc.Block())

        @block.sync
        def _(sp):
            sp.dma_start(xs[:, :], x_d).then_inc(in_x, 16)
            sp.dma_start(idx_i[:, :, :], idx_d).then_inc(in_idx, 16)
            sp.dma_start(cols[:, :], cols_d).then_inc(in_cols, 16)
            sp.dma_start(w4[:, :], w4_d).then_inc(in_w4, 16)
            sp.dma_start(wqk[:, :, :], wqk_d).then_inc(in_wqk, 16)
            sp.dma_start(wv[:, :, :], wv_d).then_inc(in_wv, 16)
            sp.dma_start(brow[:, :, :], brow_d.partition_broadcast(128)).then_inc(in_brow, 16)
            sp.dma_start(wout[:, :, :], wout_d).then_inc(in_wout, 16)
            sp.dma_start(wup[:, :, :], wup_d).then_inc(in_small, 16)
            sp.dma_start(wo[:, :, :], wo_d).then_inc(in_small, 16)
            sp.dma_start(l3w1[:, :, :], l3w1_d).then_inc(in_small, 16)
            sp.dma_start(l3w2[:, :], l3w2_d).then_inc(in_small, 16)
            sp.dma_start(b31[:, :], b31_d.partition_broadcast(128)).then_inc(in_small, 16)
            sp.wait_ge(rad_mm, 12)
            sp.wait_ge(split_ready, 2 * SB)
            for j in range(4):
                sp.dma_start(w1[:, j, :, :], w1_d[:, j, :, :]).then_inc(in_w1[j], 16)
            sp.wait_ge(counts_mm, 1)
            for j in range(4):
                sp.dma_start(w2[:, 4 * j:4 * j + 4, :], w2_d[:, 4 * j:4 * j + 4, :]).then_inc(in_w2[j], 16)
            sp.wait_ge(qk_mm, 2)
            sp.dma_start(src_i[0][:, :], srow_d[0:E // 2].partition_broadcast(128)).then_inc(in_srow[0], 16)
            sp.wait_ge(up_mm, F0B)
            sp.dma_start(src_i[1][:, :], srow_d[E // 2:E].partition_broadcast(128)).then_inc(in_srow[1], 16)
            sp.wait_ge(down_mm, 2)
            sp.wait_ge(gathered, EC // 2)
            sp.dma_start(l2w1[:, :, :], l2w1_d).then_inc(in_l2w1, 16)
            sp.wait_ge(prod_ready, F2B)
            sp.dma_start(l2w2[:, :, :], l2w2_d).then_inc(in_l2w2, 16)
            for g in range(2):
                half = slice(g * 256, g * 256 + 256)
                sp.wait_ge(out_ready, g + 1)
                sp.dma_start(out_d[:, half], un[:, half]).then_inc(out_sent, 16)
            sp.wait_ge(out_sent, 32)

        @block.gpsimd
        def _(pool):
            pool.memset(neghalf[:, :], -0.5).then_inc(consts_ready, 1)
            pool.iota(iota_row[:, :], pattern=[[1, 128]], base=0, channel_multiplier=0,
                      allow_small_or_imprecise_dtypes=True).then_inc(consts_ready, 1)
            pool.iota(iota_p[:, :], pattern=[[1, 1]], base=0, channel_multiplier=1,
                      allow_small_or_imprecise_dtypes=True).then_inc(consts_ready, 1)
            pool.memset(ident[:, :], 0.0).then_inc(zeroed, 1)
            pool.wait_ge(zeroed, 1)
            pool.affine_select(out=ident[:, :], in_=ident[:, :], compare_op=ALU.not_equal, fill=1.0,
                               base=0, pattern=[[-1, 128]], channel_multiplier=1).then_inc(consts_ready, 1)

            def root(n):
                pool.wait_ge(var_ready, n)
                pool.tensor_tensor(rstd[:, :], ve[:, :], neghalf[:, :], ALU.pow).then_inc(rstd_ready, 1)

            pool.wait_ge(consts_ready, 4)
            root(1)
            root(2)
            pool.wait_ge(idx_cast, 1)
            for c in range(EC - POOL_OH, EC):
                pool.tensor_scalar(ohd[:, c, :], iota_row[:, :], end_f[:, 1, c:c + 1], None,
                                   ALU.is_equal).then_inc(onehots_pool, 1)
            pool.wait_ge(h_ready, 1)
            pool.wait_ge(in_brow, 16)
            pool.tensor_tensor(un[:, :], hn[:, :], brow[:, 0, :], ALU.add).then_inc(hb_ready, 1)
            pool.tensor_tensor(xs[:, :], xs[:, :], brow[:, 1, :], ALU.add).then_inc(hb_ready, 1)
            root(3)
            pool.wait_ge(xr_ready, 1)
            pool.wait_ge(hb_ready, 2)
            pool.tensor_tensor(xs[:, :], xs[:, :], xr[:, :], ALU.add).then_inc(hb_ready, 1)
            pool.wait_ge(proj_mm, 1)
            for c in range(EC):
                pool.tensor_scalar(oh[:, c, :], iota_row[:, :], end_f[:, 1, c:c + 1], None,
                                   ALU.is_equal).then_inc(oh_ready, 1)

            def select(c):
                g, i = divmod(c, EC // 2)
                pool.tensor_scalar(gsel[g][:, i, :], src_i[g][:, i * 128:(i + 1) * 128], iota_p[:, :], None, ALU.is_equal).then_inc(gsel_ready, 1)

            pool.wait_ge(in_srow[0], 16)
            for c in range(EC // 2):
                select(c)
            root(4)
            for c in range(T_MLP, T_MLP + Y0_POOL):
                pool.wait_ge(*taken(c))
                pool.tensor_scalar(tpw[:, c, 128:384], tpw[:, c, 128:384], cols[:, C_Y + 4 * c:C_Y + 4 * c + 1], None,
                                   ALU.mult).then_inc(y0_pool, 1)
            pool.wait_ge(in_srow[1], 16)
            for c in range(EC):
                b = c % UNROLL
                pool.wait_ge(ac_rounded, c + 1)
                pool.tensor_tensor(ac_lo[b][:, :], prod[b][:, 1:5, :].rearrange("p q u -> p (q u)"), ac_hi[b][:, :],
                                   ALU.subtract).then_inc(ac_left, 1)
                if c % 3 < 2 and EC // 2 + c // 3 * 2 + c % 3 < EC:
                    select(EC // 2 + c // 3 * 2 + c % 3)
            root(5)
            pool.wait_ge(h_ready, 5)
            pool.tensor_tensor(xs[:, :], xs[:, :], brow[:, 2, :], ALU.add).then_inc(hb2_ready, 1)
            pool.wait_ge(rstd_ready, 5)
            pool.tensor_scalar(un[:, :], hn[:, :], rstd[:, :], None, ALU.mult).then_inc(hb2_ready, 1)
            pool.wait_ge(hb2_ready, 2)
            pool.tensor_tensor(xs[:, :], xs[:, :], un[:, :], ALU.add).then_inc(hb2_ready, 1)
            root(6)

        @block.scalar
        def _(act):
            act.dma_start(feat_wm1[:, :], feat_d).then_inc(in_feat, 16)
            act.dma_start(wm23[:, :, :], wm23_d).then_inc(in_wm, 16)
            act.preload_act_table(ACT.Silu)

            def radial(layer):
                for s in range(SB):
                    act.wait_ge(rad_mm, SB * layer + s + 1)
                    scale = RB ** -0.5 if layer == 0 else SILU_2MOM * HID ** -0.5
                    act.activation(hid[layer % 2][:, s, :], P[4 + s][:, :], ACT.Silu,
                                   scale=scale).then_inc(rad_act, 1)

            def tpw_out(cs):
                for c in cs:
                    if c not in by_dve:
                        act.wait_ge(tpw_mm, c + 1)
                        act.activation(tpw[:, c, :], P[4 + c % 4][:, :], ACT.Copy,
                                       scale=PATH_SCALE).then_inc(tpw_act, 1)

            def xn_out(w, b):
                for j in (2, 3):
                    act.activation(hT[:, j, :], P[1][:, (j - 2) * 128:(j - 1) * 128], ACT.Identity,
                                   scale=cols[:, w + j:w + j + 1],
                                   bias=cols[:, b + j:b + j + 1]).then_inc(hT_act, 1)

            radial(0)
            act.wait_ge(in_cols, 16)
            act.wait_ge(hT_ready, 1)
            xn_out(C_LN1W, C_LN1B)
            radial(1)
            radial(2)
            act.wait_ge(rad_act, 3 * SB)
            for s in range(SB):
                act.activation(stk[s][0:64, 0, :], hid[0][0:64, s, :], ACT.Copy).then_inc(hi_ready, 1)
                act.activation(stk[s][64:128, 1, :], hid[0][64:128, s, :], ACT.Copy).then_inc(hi_ready, 1)
            act.preload_act_table(ACT.Exp)
            tpw_out(range(0, 1))
            for g in range(2):
                act.wait_ge(max_ready, g + 1)
                for b in range(4):
                    s = 4 * g + b
                    act.activation(prob[:, s, :], prob[:, s, :], ACT.Exp, bias=smax[:, s:s + 1],
                                   accum_out=ssum[:, s:s + 1]).then_inc(exp_ready, 1)
            act.wait_ge(v_mm, 1)
            act.activation(vn[:, :], P[0][:, :], ACT.Copy).then_inc(v_ready, 1)
            tpw_out(range(1, T_SOFT))
            act.wait_ge(probT_mm, 2)
            act.activation(probT[:, 4:8, :], P[1][:, :], ACT.Copy).then_inc(probT_act, 1)
            tpw_out(range(T_SOFT, T_NORM2 - 2))
            act.wait_ge(hT_ready, 2)
            xn_out(C_LN2W, C_LN2B)
            tpw_out(range(T_NORM2 - 2, T_MLP))
            for j in range(1, F0B, 2):
                act.wait_ge(up_mm, j + 1)
                act.activation(hid0T[:, j, :], P[j % 3][:, 0:128], ACT.Relu,
                               bias=cols[:, C_B1 + j:C_B1 + j + 1]).then_inc(up_act, 1)
            tpw_out(range(T_MLP, T_NORM3))
            act.wait_ge(hT_ready, 3)
            act.activation(hT[:, 2:4, :], P[1][:, 0:256], ACT.Copy).then_inc(hT_act, 1)
            def first_product(c, k):
                act.wait_ge(gathered, c + 1)
                act.activation(tdot[k][:, :], P[k][:, 128:256], ACT.Copy, scale=y_of(c, 1)).then_inc(t0_ready, 1)

            def weigh(c, k, first):
                if not first:
                    act.wait_ge(scattered, c - UNROLL + 1)
                one = oh[:, bass.ds(c, 1), :].rearrange("p a n -> p (a n)").bitcast(f32)
                for m in range(3):
                    last = act.activation(ysel[k][:, m, :], one, ACT.Copy, scale=y_of(c, m + 1))
                last.then_inc(ysel_ready, 1)

            def rounded(c, k):
                act.wait_ge(ac_ready, c + 1)
                act.activation(ac_hi[k][:, :], prod[k][:, 1:5, :].rearrange("p q u -> p (q u)"),
                               ACT.Copy).then_inc(ac_rounded, 1)

            act.wait_ge(oh_ready, EC)
            weigh(0, 0, True)
            tpw_out(range(T_NORM3, EC))
            first_product(0, 0)
            weigh(1, 1, True)
            first_product(1, 1)
            for k in range(2, UNROLL):
                rounded(k - 2, k - 2)
                first_product(k, k)
                weigh(k, k, True)
            rounded(UNROLL - 2, UNROLL - 2)
            with act.Fori(1, EC // UNROLL) as i:
                for k in range(UNROLL):
                    first_product(i * UNROLL + k, k)
                    weigh(i * UNROLL + k, k, False)
                    rounded(i * UNROLL + (k - 1), (k - 1) % UNROLL)
            rounded(EC - 1, UNROLL - 1)
            act.wait_ge(bd_done, 1)
            act.activation(msg[:, 4:7, :], P[7][:, 0:384], ACT.Copy).then_inc(msg_act, 1)
            act.activation(msg[:, 7, :], P[7][:, 384:512], ACT.Copy, scale=3.0 ** -0.5).then_inc(msg_act, 1)
            act.wait_ge(msgT_mm, 1)
            act.activation(msgT[:, 4:8, :], P[1][:, :], ACT.Copy).then_inc(msgT_act, 1)
            act.wait_ge(rst_mm, 2)
            act.activation(hT[:, 2:4, :], P[1][:, 0:256], ACT.Copy).then_inc(rst_ready, 1)
            act.wait_ge(adjT_mm, 1)
            act.activation(cnt_ds[:, :], P[7][:, 0:128], ACT.Copy).then_inc(adjT_ready, 1)
            for j in range(1, F2B, 2):
                act.wait_ge(up2_mm, j + 1)
                act.activation(hid2T[:, j, :], P[(1, 2, 4, 5)[j % 4]][:, 0:128], ACT.Relu,
                               bias=cols[:, C_L2B1 + j:C_L2B1 + j + 1]).then_inc(up2_act, 1)
            act.wait_ge(hT_ready, 4)
            act.activation(hT[:, 2:4, :], P[1][:, 0:256], ACT.Copy).then_inc(hT_act, 1)

        @block.vector
        def _(dve):
            chained = [0]

            def link(ins):
                chained[0] += 1
                ins.then_inc(dve_chain, 1)
                dve.wait_ge(dve_chain, chained[0])

            def stat(parts):
                link(dve.bn_aggr(mv[:, :], stats[:, 0:parts, :].rearrange("p n s -> p (n s)")))
                dve.tensor_scalar(ve[:, :], mv[:, 1:2], EPS, None, ALU.add).then_inc(var_ready, 1)

            def relu_norm(n):
                link(dve.bn_stats(stats[:, 0, :], xs[:, :]))
                stat(1)
                link(dve.tensor_scalar(hn[:, :], xs[:, :], mv[:, 0:1], 0.0, ALU.subtract, ALU.max))
                dve.wait_ge(rstd_ready, n)
                ins = dve.tensor_scalar(hn[:, :], hn[:, :], rstd[:, :], None, ALU.mult)
                ins.then_inc(h_ready, 1)

            def relu_center(parts):
                stat(parts)
                dve.tensor_scalar(hn[:, :], xs[:, :], mv[:, 0:1], 0.0, ALU.subtract, ALU.max).then_inc(h_ready, 1)

            def residual(bank_a, bank_b, made, before):
                for g in range(2):
                    half = slice(g * 256, g * 256 + 256)
                    dve.wait_ge(made, g + 1)
                    dve.tensor_tensor(xs[:, half], P[(bank_a, bank_b)[g]][:, 0:256], xs[:, half],
                                      ALU.add).then_inc(res_ready, 1)
                for g in range(2):
                    dve.wait_ge(res_ready, before + g + 1)
                    dve.bn_stats(stats[:, g, :], xs[:, g * 256:g * 256 + 256]).then_inc(dve_chain, 1)
                chained[0] += 2
                dve.wait_ge(dve_chain, chained[0])

            def affine_norm(src, n):
                link(dve.bn_stats(stats[:, 0, :], src))
                stat(1)
                dve.wait_ge(rstd_ready, n)
                dve.tensor_scalar(zn[:, :], src, mv[:, 0:1], rstd[:, :], ALU.subtract, ALU.mult)\
                   .then_inc(h_ready, 1)

            def tpw_out(cs):
                for c in cs:
                    if c not in by_dve:
                        continue
                    dve.wait_ge(tpw_mm, c + 1)
                    if c < T_MLP:
                        dve.tensor_scalar(tpw[:, c, :], P[4 + c % 4][:, :], PATH_SCALE, None,
                                          ALU.mult).then_inc(tpw_dve, 1)
                    else:
                        w, q = path_views(c)
                        dve.tensor_scalar(w[:, 1:3, :], q[:, 1:3, :], y0s[:, c:c + 1], None, ALU.mult)
                        dve.tensor_scalar(w[:, 0:4:3, :], q[:, 0:4:3, :], PATH_SCALE, None, ALU.mult).then_inc(tpw_dve, 1)

            def times_y0(c):
                dve.wait_ge(*taken(c))
                dve.tensor_scalar(tpw[:, c, 128:384], tpw[:, c, 128:384], cols[:, C_Y + 4 * c:C_Y + 4 * c + 1], None,
                                  ALU.mult).then_inc(y0_in, 1)

            dve.memset(warm[:, :], 0.0).then_inc(warm_ready, 1)
            dve.wait_ge(in_x, 16)
            relu_norm(1)
            dve.wait_ge(h_ready, 1)
            affine_norm(hn[:, :], 2)
            dve.wait_ge(consts_ready, 4)
            link(dve.tensor_copy(iota_rb[:, :], iota_row[:, :]))
            dve.wait_ge(in_idx, 16)
            dve.tensor_copy(end_f[:, :, :], idx_i[:, :, :]).then_inc(idx_cast, 1)
            dve.wait_ge(idx_cast, 1)

            def onehot(k, t, cs):
                for c in cs:
                    dve.tensor_scalar(t[:, c, :], iota_rb[:, :], end_f[:, k, c:c + 1], None,
                                      ALU.is_equal).then_inc(onehots, 1)

            onehot(0, ohs, range(12))
            dve.wait_ge(in_cols, 16)
            dve.wait_ge(hT_ready, 1)
            for j in (0, 1):
                dve.tensor_scalar(hT[:, j, :], P[0][:, j * 128:(j + 1) * 128],
                                  cols[:, C_LN1W + j:C_LN1W + j + 1], cols[:, C_LN1B + j:C_LN1B + j + 1],
                                  ALU.mult, ALU.add).then_inc(hT_dve, 1)
            dve.tensor_scalar(y0s[:, :], cols[:, C_Y:C_Y + 4 * EC:4], PATH_SCALE, None, ALU.mult).then_inc(y0s_ready, 1)
            dve.wait_ge(in_w4, 16)
            link(dve.tensor_copy(w4hi[:, :], w4[:, :]))
            dve.tensor_tensor(w4lo[:, :], w4[:, :], w4hi[:, :], ALU.subtract).then_inc(w4_split, 1)
            onehot(0, ohs, range(12, EC))
            onehot(1, ohd, range(EC - POOL_OH))
            for s in range(SB):
                h = hid[0][:, s, :]
                dve.wait_ge(hi_ready, 2 * s + 1)
                dve.tensor_tensor(stk[s][64:128, 0, :], h[0:64, :], stk[s][0:64, 0, :],
                                  ALU.subtract).then_inc(split_ready, 1)
                dve.wait_ge(hi_ready, 2 * s + 2)
                dve.tensor_tensor(stk[s][0:64, 1, :], h[64:128, :], stk[s][64:128, 1, :],
                                  ALU.subtract).then_inc(split_ready, 1)
            for g in range(2):
                dve.wait_ge(qk_mm, g + 1)
                dve.tensor_tensor(qkT[:, 4 * g:4 * g + 4, :],
                                  P[2 + g][:, :].rearrange("p (b n) -> p b n", b=4),
                                  cols[:, C_BQK + 4 * g:C_BQK + 4 * g + 4].unsqueeze(2).broadcast_to([128, 4, 128]),
                                  ALU.add).then_inc(qk_ready, 1)
            dve.wait_ge(counts_mm, 1)
            link(dve.tensor_tensor(adj[:, :], P[1][:, 0:128], ident[:, :], ALU.add))
            dve.tensor_scalar(eps1[:, :], cols[:, C_EPS:C_EPS + 1], 1.0, None, ALU.add).then_inc(dve_chain, 1)
            link(dve.tensor_scalar(mask[:, :], adj[:, :], 0.5, NEG, ALU.is_lt, ALU.mult))
            chained[0] += 1
            dve.wait_ge(dve_chain, chained[0])
            dve.scalar_tensor_tensor(out=cnt_sd[:, :], in0=ident[:, :], scalar=eps1[:, :], in1=P[1][:, 0:128],
                                     op0=ALU.mult, op1=ALU.add).then_inc(counts_ready, 1)
            for g in range(2):
                dve.wait_ge(scores_mm, g + 1)
                link(dve.scalar_tensor_tensor(out=prob[:, 4 * g:4 * g + 4, :],
                                              in0=P[2 + g][:, :].rearrange("p (b n) -> p b n", b=4),
                                              scalar=DH ** -0.5,
                                              in1=mask[:, :].unsqueeze(1).broadcast_to([128, 4, 128]),
                                              op0=ALU.mult, op1=ALU.add))
                link(dve.tensor_reduce(smax[:, 4 * g:4 * g + 4], prob[:, 4 * g:4 * g + 4, :], AX.X, ALU.max))
                dve.tensor_scalar(smax[:, 4 * g:4 * g + 4], smax[:, 4 * g:4 * g + 4], -1.0, None,
                                  ALU.mult).then_inc(max_ready, 1)
            tpw_out(range(0, T_SOFT))
            for g in range(2):
                dve.wait_ge(exp_ready, 4 * g + 4)
                link(dve.reciprocal(srec[:, 4 * g:4 * g + 4], ssum[:, 4 * g:4 * g + 4]))
                for b in range(4):
                    s = 4 * g + b
                    dve.tensor_scalar(prob[:, s, :], prob[:, s, :], srec[:, s:s + 1], None,
                                      ALU.mult).then_inc(prob_ready, 1)
            dve.wait_ge(probT_mm, 1)
            dve.tensor_copy(probT[:, 0:4, :], P[0][:, :].rearrange("p (b n) -> p b n", b=4)).then_inc(probT_dve, 1)
            tpw_out(range(T_SOFT, T_ATTN))
            dve.wait_ge(o_mm, 1)
            dve.tensor_tensor(oT[:, :, :], P[2][:, :].rearrange("p (b n) -> p b n", b=4),
                              cols[:, C_BV:C_BV + 4].unsqueeze(2).broadcast_to([128, 4, 128]),
                              ALU.add).then_inc(o_ready, 1)
            tpw_out(range(T_ATTN, T_PROJ))
            dve.wait_ge(proj_mm, 1)
            dve.wait_ge(hb_ready, 1)
            dve.tensor_tensor(xr[:, :], P[3][:, :], un[:, :], ALU.add).then_inc(xr_ready, 1)
            dve.wait_ge(xr_ready, 1)
            affine_norm(xr[:, :], 3)
            dve.wait_ge(hT_ready, 2)
            for j in (0, 1):
                dve.tensor_scalar(hT[:, j, :], P[0][:, j * 128:(j + 1) * 128],
                                  cols[:, C_LN2W + j:C_LN2W + j + 1], cols[:, C_LN2B + j:C_LN2B + j + 1],
                                  ALU.mult, ALU.add).then_inc(hT_dve, 1)
            tpw_out(range(T_PROJ, T_MLP))
            for j in range(0, F0B, 2):
                dve.wait_ge(up_mm, j + 1)
                dve.tensor_scalar(hid0T[:, j, :], P[j % 3][:, 0:128], cols[:, C_B1 + j:C_B1 + j + 1], 0.0,
                                  ALU.add, ALU.max).then_inc(up_dve, 1)
                for c in range(3 * j // 2, min(3 * j // 2 + 3, T_MLP)):
                    times_y0(c)
            dve.wait_ge(hb_ready, 3)
            residual(3, 4, down_mm, 0)

            relu_center(2)
            dve.wait_ge(hT_ready, 3)
            dve.tensor_copy(hT[:, 0:2, :], P[0][:, 0:256].rearrange("p (b n) -> p b n", b=2)).then_inc(hT_dve, 1)
            dve.wait_ge(rstd_ready, 4)
            link(dve.tensor_scalar(nscale[:, :], rstd[:, :], MUL ** -0.5, None, ALU.mult))
            tpw_out(range(T_MLP, T_LIFT))
            dve.wait_ge(lift_mm, 1)
            link(dve.tensor_scalar(xup_hi[:, :], P[2][:, :], nscale[:, :], None, ALU.mult))
            dve.scalar_tensor_tensor(out=xup_lo[:, :], in0=P[2][:, :], scalar=nscale[:, :], in1=xup_hi[:, :],
                                     op0=ALU.mult, op1=ALU.subtract).then_inc(lift_ready, 1)

            def messages(c, k, first):
                g, p, t = P[k], prod[k], tdot[k]
                w = tpw[:, bass.ds(c, 1), :].rearrange("p a (q u) -> p (a q) u", q=4)
                dve.wait_ge(t0_ready, c + 1)
                if not first:
                    dve.wait_ge(scattered, c - UNROLL + 1)
                dve.scalar_tensor_tensor(out=t[:, :], in0=g[:, 256:384], scalar=y_of(c, 2), in1=t[:, :],
                                         op0=ALU.mult, op1=ALU.add).then_inc(t_steps, 1)
                dve.tensor_tensor(p[:, 0:2, :], g[:, 0:128].unsqueeze(1).broadcast_to([128, 2, 128]),
                                  w[:, 0:2, :], ALU.mult)
                dve.wait_ge(t_steps, 2 * c + 1)
                dve.scalar_tensor_tensor(out=t[:, :], in0=g[:, 384:512], scalar=y_of(c, 3), in1=t[:, :],
                                         op0=ALU.mult, op1=ALU.add).then_inc(t_steps, 1)
                dve.tensor_tensor(p[:, 2:5, :], g[:, 128:512].rearrange("p (m u) -> p m u", m=3),
                                  w[:, 2:3, :].broadcast_to([128, 3, 128]), ALU.mult).then_inc(ac_ready, 1)
                dve.wait_ge(t_steps, 2 * c + 2)
                dve.tensor_tensor(p[:, 5, :], t[:, :], w[:, 3, :], ALU.mult).then_inc(prod_ready, 1)

            for c in range(T_MLP + Y0_POOL, T_LIFT + 2):
                if c not in by_dve:
                    times_y0(c)
            dve.wait_ge(y0_in, UNROLL)
            for k in range(UNROLL):
                messages(k, k, True)
            for c in range(T_LIFT + 2, EC):
                if c not in by_dve:
                    times_y0(c)
            dve.wait_ge(tpw_dve, len(by_dve))
            dve.wait_ge(y0_in, EC - Y0_POOL - sum(c >= T_MLP for c in by_dve))
            dve.wait_ge(y0_pool, Y0_POOL)
            with dve.Fori(1, EC // UNROLL) as i:
                for k in range(UNROLL):
                    messages(i * UNROLL + k, k, False)
            dve.wait_ge(scattered, EC)
            for g in range(2):
                dve.tensor_copy(msg[:, 2 * g:2 * g + 2, :],
                                P[6][:, 256 * g:256 * g + 256].rearrange("p (b n) -> p b n", b=2)).then_inc(msg_dve, 1)
            dve.wait_ge(msgT_mm, 2)
            dve.tensor_copy(msgT[:, 0:4, :], P[0][:, :].rearrange("p (b n) -> p b n", b=4)).then_inc(msgT_dve, 1)
            final = (2 * MUL) ** -0.5 / AVG_NEIGH
            plane = [xs[:, 0:128]] + [xs[:, 128 + m:512:3] for m in range(3)]
            for n in range(5):
                if n < 4:
                    dve.wait_ge(l1_mm, n + 1)
                    dve.scalar_tensor_tensor(out=plane[n], in0=P[2 + n][:, 0:128], scalar=final, in1=plane[n],
                                             op0=ALU.mult, op1=ALU.add).then_inc(l1_done, 1)
                if n >= 1:
                    dve.wait_ge(l1_done, n)
                    dve.bn_stats(stats[:, n - 1, :], plane[n - 1]).then_inc(dve_chain, 1)
            chained[0] += 4
            dve.wait_ge(dve_chain, chained[0])

            relu_center(4)
            dve.wait_ge(rstd_ready, 5)
            dve.tensor_scalar(cnt_n[:, :], cnt_sd[:, :], rstd[:, :], None, ALU.mult).then_inc(h_ready, 1)
            dve.wait_ge(rst_mm, 1)
            dve.tensor_copy(hT[:, 0:2, :], P[0][:, 0:256].rearrange("p (b n) -> p b n", b=2)).then_inc(rst_ready, 1)
            for j in range(0, F2B, 2):
                dve.wait_ge(up2_mm, j + 1)
                dve.tensor_scalar(hid2T[:, j, :], P[(1, 2, 4, 5)[j % 4]][:, 0:128], cols[:, C_L2B1 + j:C_L2B1 + j + 1], 0.0,
                                  ALU.add, ALU.max).then_inc(up2_dve, 1)
            dve.wait_ge(hb2_ready, 3)
            residual(3, 6, down2_mm, 2)

            relu_center(2)
            dve.memset(r3[:, F3:F3 + 1], 1.0).then_inc(r3_ready, 1)
            dve.wait_ge(hT_ready, 4)
            dve.tensor_copy(hT[:, 0:2, :], P[0][:, 0:256].rearrange("p (b n) -> p b n", b=2)).then_inc(hT_dve, 1)
            dve.wait_ge(rstd_ready, 6)
            dve.wait_ge(r3_mm, 1)
            link(dve.scalar_tensor_tensor(out=r3[:, 0:F3], in0=P[2][:, 0:F3], scalar=rstd[:, :], in1=b31[:, :],
                                          op0=ALU.mult, op1=ALU.add))
            dve.tensor_scalar(r3[:, 0:F3], r3[:, 0:F3], 0.0, None, ALU.max).then_inc(r3_ready, 1)
            dve.wait_ge(z3_mm, 1)
            dve.tensor_copy(zT[:, :], P[4][0:F3 + 1, 0:128]).then_inc(z3_ready, 1)
            for g in range(2):
                half = slice(g * 256, g * 256 + 256)
                dve.wait_ge(out_mm, g + 1)
                dve.tensor_tensor(un[:, half], P[5 + g][:, 0:256], xs[:, half], ALU.add).then_inc(out_ready, 1)

        @block.tensor
        def _(pe):
            def transposes(src, n, dsts, signal):
                for j in range(n):
                    last = pe.transpose(dsts[j], src[j], ident[:, :])
                last.then_inc(signal, 1)

            def radial(layer):
                for s in range(SB):
                    if layer == 0:
                        pe.matmul(P[4 + s][:, :], feat_wm1[:, SB * HALF:], feat_wm1[:, s * HALF:(s + 1) * HALF],
                                  start=True, stop=True).then_inc(rad_mm, 1)
                    else:
                        pe.wait_ge(rad_act, SB * (layer - 1) + s + 1)
                        pe.matmul(P[4 + s][:, :], wm23[:, layer - 1, :], hid[(layer - 1) % 2][:, s, :],
                                  start=True, stop=True).then_inc(rad_mm, 1)

            def paths(cs):
                for c in cs:
                    s, half, col = c // SBC, c % SBC // 4, c % 4 * 128
                    if c >= 4:
                        pe.wait_ge(*taken(c - 4))
                    if c == -(-T_MLP // 4) * 4:
                        pe.wait_ge(res_ready, 2)
                    h = stk[s][:, half, col:col + 128]
                    pe.matmul(P[4 + c % 4][:, :], h, w4hi[:, :], start=True, stop=False)
                    pe.matmul(P[4 + c % 4][:, :], h, w4lo[:, :], start=False, stop=True).then_inc(tpw_mm, 1)

            def keep_clock(n):
                for _ in range(n):
                    pe.matmul(P[7][:, :], warm[:, 0:128], warm[:, :], start=True, stop=True)

            def blocks(src):
                return [src[:, j * 128:(j + 1) * 128] for j in range(4)]

            two_banks = [P[j // 2][:, (j % 2) * 128:(j % 2 + 1) * 128] for j in range(4)]

            pe.wait_ge(warm_ready, 1)
            for _ in range(WARM):
                pe.matmul(P[0][:, :], warm[:, 0:128], warm[:, :], start=True, stop=True)
            pe.wait_ge(in_feat, 16)
            radial(0)
            pe.wait_ge(consts_ready, 4)
            pe.wait_ge(h_ready, 2)
            transposes(blocks(zn), 4, two_banks, hT_ready)
            pe.wait_ge(in_wm, 16)
            radial(1)
            radial(2)
            pe.wait_ge(in_wqk, 16)
            pe.wait_ge(hT_act, 2)
            pe.wait_ge(hT_dve, 2)
            for b in range(8):
                for j in range(DB):
                    last = pe.matmul(P[2 + b // 4][:, b % 4 * 128:(b % 4 + 1) * 128], wqk[:, j, b * 128:(b + 1) * 128],
                                     hT[:, j, :], start=j == 0, stop=j == DB - 1)
                if b % 4 == 3:
                    last.then_inc(qk_mm, 1)
            pe.wait_ge(onehots, 2 * EC - POOL_OH)
            pe.wait_ge(onehots_pool, POOL_OH)
            for c in range(EC):
                last = pe.matmul(P[1][:, 0:128], ohs[:, c, :], ohd[:, c, :], start=c == 0, stop=c == EC - 1)
            last.then_inc(counts_mm, 1)
            pe.wait_ge(qk_ready, 2)
            for g in range(2):
                rows = slice(64 * g, 64 * g + 64)
                for b in range(4):
                    last = pe.matmul(P[2 + g][:, b * 128:(b + 1) * 128], qkT[rows, b, :], qkT[rows, 4 + b, :],
                                     start=True, stop=True)
                last.then_inc(scores_mm, 1)
            pe.wait_ge(w4_split, 1)
            pe.wait_ge(split_ready, 2 * SB)
            paths(range(0, T_V))
            pe.wait_ge(in_wv, 16)
            for j in range(DB):
                last = pe.matmul(P[0][:, :], hT[:, j, :], wv[:, j, :], start=j == 0, stop=j == DB - 1)
            last.then_inc(v_mm, 1)
            paths(range(T_V, T_SOFT))
            pe.wait_ge(v_ready, 1)
            pe.wait_ge(counts_ready, 1)
            for g in range(2):
                for b in range(4):
                    pe.wait_ge(prob_ready, 4 * g + b + 1)
                    last = pe.transpose(P[g][:, b * 128:(b + 1) * 128], prob[:, 4 * g + b, :], ident[:, :])
                last.then_inc(probT_mm, 1)
            paths(range(T_SOFT, T_ATTN))
            for g in range(2):
                if g == 0:
                    pe.wait_ge(probT_dve, 1)
                else:
                    pe.wait_ge(probT_act, 1)
                for b in range(4):
                    h = 2 * b + g
                    last = pe.matmul(P[2][64 * g:64 * g + 64, b * 128:(b + 1) * 128], vn[:, h * DH:(h + 1) * DH],
                                     probT[:, 4 * g + b, :], start=True, stop=True)
            last.then_inc(o_mm, 1)
            paths(range(T_ATTN, T_PROJ))
            pe.wait_ge(o_ready, 1)
            pe.wait_ge(in_wout, 16)
            for j in range(DB):
                last = pe.matmul(P[3][:, :], oT[:, j, :], wout[:, j, :], start=j == 0, stop=j == DB - 1)
            last.then_inc(proj_mm, 1)
            paths(range(T_PROJ, T_NORM2))
            pe.wait_ge(h_ready, 3)
            transposes(blocks(zn), 4, two_banks, hT_ready)
            paths(range(T_NORM2, T_MLP))
            pe.wait_ge(hT_act, 4)
            pe.wait_ge(hT_dve, 4)

            def down(j):
                if j % 4 == 0:
                    pe.wait_ge(in_w2[j // 4], 16)
                if j % 2:
                    pe.wait_ge(up_act, j // 2 + 1)
                else:
                    pe.wait_ge(up_dve, j // 2 + 1)
                for g in range(2):
                    last = pe.matmul(P[3 + g][:, 0:256], hid0T[:, j, :], w2[:, j, g * 256:g * 256 + 256],
                                     start=j == 0, stop=j == F0B - 1)
                    if j == F0B - 1:
                        last.then_inc(down_mm, 1)

            for f in range(F0B):
                if f % 4 == 0:
                    pe.wait_ge(in_w1[f // 4], 16)
                for j in range(DB):
                    last = pe.matmul(P[f % 3][:, 0:128], w1[:, f // 4, j, f % 4 * 128:(f % 4 + 1) * 128],
                                     hT[:, j, :], start=j == 0, stop=j == DB - 1, skip_group_check=True)
                last.then_inc(up_mm, 1)
                if f == 2:
                    pe.wait_ge(*taken(T_MLP - 1))
                if f >= 2:
                    down(f - 2)
            down(F0B - 2)
            down(F0B - 1)
            paths(range(T_MLP, T_NORM3))

            pe.wait_ge(in_small, 80)
            pe.wait_ge(h_ready, 4)
            views = [hn[:, 0:128]] + [hn[:, 128 + m:512:3] for m in range(3)]
            transposes(views, 4, two_banks, hT_ready)
            paths(range(T_NORM3, T_LIFT))
            pe.wait_ge(hT_act, 5)
            pe.wait_ge(hT_dve, 5)
            for j in range(4):
                last = pe.matmul(P[2][:, j * 128:(j + 1) * 128], hT[:, j, :], wup[:, min(j, 1), :], start=True, stop=True)
            last.then_inc(lift_mm, 1)
            paths(range(T_LIFT, EC))
            pe.wait_ge(lift_ready, 1)

            def gather(c, k, first):
                pe.wait_ge(gsel_ready, c + 1)
                if not first:
                    pe.wait_ge(prod_ready, c - UNROLL + 1)
                sel = gsel[c // (EC // 2)][:, c % (EC // 2), :]
                pe.matmul(P[k][:, :], sel, xup_hi[:, :], start=True, stop=False)
                pe.matmul(P[k][:, :], sel, xup_lo[:, :], start=False, stop=True).then_inc(gathered, 1)

            def scatter(c, k):
                p, first, last = prod[k], c == 0, c == EC - 1
                pe.wait_ge(ysel_ready, c + 1)
                pe.wait_ge(prod_ready, c + 1)
                for m in range(3):
                    pe.matmul(P[7][:, m * 128:(m + 1) * 128], ysel[k][:, m, :], p[:, 0, :],
                              start=first and m == 0, stop=last, skip_group_check=True)
                d = pe.matmul(P[7][:, 384:512], oh[:, c, :].bitcast(f32), p[:, 5, :], start=False, stop=last,
                              skip_group_check=True)
                if last:
                    d.then_inc(bd_done, 1)
                pe.wait_ge(ac_rounded, c + 1)
                pe.matmul(P[6][:, :], oh[:, c, :], ac_hi[k][:, :], start=first, stop=False,
                          skip_group_check=True)
                pe.wait_ge(ac_left, c + 1)
                pe.matmul(P[6][:, :], oh[:, c, :], ac_lo[k][:, :], start=False, stop=last,
                          skip_group_check=True).then_inc(scattered, 1)

            pe.wait_ge(oh_ready, EC)
            for c in range(EC + LAG):
                if c == LAG:
                    pe.wait_ge(*taken(EC - 2))
                    pe.wait_ge(*taken(EC - 1))
                if c < EC:
                    gather(c, c % UNROLL, c < UNROLL)
                if c >= LAG:
                    scatter(c - LAG, (c - LAG) % UNROLL)
            pe.wait_ge(msg_act, 2)
            for j in range(4):
                last = pe.transpose(P[1][:, j * 128:(j + 1) * 128], msg[:, 4 + j, :], ident[:, :])
            last.then_inc(msgT_mm, 1)
            for j in range(4):
                if j % 2 == 0:
                    pe.wait_ge(msg_dve, j // 2 + 1)
                last = pe.transpose(P[0][:, j * 128:(j + 1) * 128], msg[:, j, :], ident[:, :])
            last.then_inc(msgT_mm, 1)
            pe.wait_ge(msgT_act, 1)
            planes = ((7, 1, 0, 0), (4, 2, 1, 3), (5, 2, 2, 3), (6, 2, 3, 3))
            for n, (j, g, _, _) in enumerate(planes):
                pe.matmul(P[2 + n][:, 0:128], msgT[:, j, :], wo[:, g, :], start=True, stop=False)
            pe.wait_ge(msgT_dve, 1)
            for n, (_, _, j, g) in enumerate(planes):
                pe.matmul(P[2 + n][:, 0:128], msgT[:, j, :], wo[:, g, :], start=False, stop=True).then_inc(l1_mm, 1)

            keep_clock(10)
            pe.wait_ge(h_ready, 6)
            for j in range(DB):
                last = pe.matmul(P[j // 2][:, j % 2 * 128:(j % 2 + 1) * 128], hn[:, j * 128:(j + 1) * 128],
                                 cnt_n[:, :], start=True, stop=True)
                if j % 2:
                    last.then_inc(rst_mm, 1)
            pe.transpose(P[7][:, 0:128], adj[:, :], ident[:, :]).then_inc(adjT_mm, 1)
            pe.wait_ge(rst_ready, 2)
            pe.wait_ge(in_l2w1, 16)
            pe.wait_ge(in_l2w2, 16)
            pe.wait_ge(l1_done, 4)

            def down2(j):
                if j % 2:
                    pe.wait_ge(up2_act, j // 2 + 1)
                else:
                    pe.wait_ge(up2_dve, j // 2 + 1)
                for g in range(2):
                    last = pe.matmul(P[(3, 6)[g]][:, 0:256], hid2T[:, j, :], l2w2[:, j, g * 256:g * 256 + 256],
                                     start=j == 0, stop=j == F2B - 1)
                    if j == F2B - 1:
                        last.then_inc(down2_mm, 1)

            for f in range(F2B):
                for j in range(DB):
                    last = pe.matmul(P[(1, 2, 4, 5)[f % 4]][:, 0:128], l2w1[:, j, f * 128:(f + 1) * 128], hT[:, j, :],
                                     start=j == 0, stop=j == DB - 1, skip_group_check=True)
                last.then_inc(up2_mm, 1)
                if f >= 2:
                    down2(f - 2)
            down2(F2B - 2)
            down2(F2B - 1)

            pe.wait_ge(adjT_ready, 1)
            keep_clock(8)
            pe.wait_ge(h_ready, 7)
            transposes(blocks(hn), 4, two_banks, hT_ready)
            keep_clock(3)
            pe.wait_ge(hT_dve, 6)
            pe.wait_ge(hT_act, 6)
            for j in range(DB):
                last = pe.matmul(P[2][:, 0:F3], hT[:, j, :], l3w1[:, j, :], start=j == 0, stop=j == DB - 1)
            last.then_inc(r3_mm, 1)
            keep_clock(4)
            pe.wait_ge(r3_ready, 2)
            pe.matmul(P[4][0:F3 + 1, 0:128], r3[:, :], cnt_ds[:, :], start=True, stop=True).then_inc(z3_mm, 1)
            keep_clock(3)
            pe.wait_ge(z3_ready, 1)
            for g in range(2):
                pe.matmul(P[5 + g][:, 0:256], zT[:, :], l3w2[:, g * 256:g * 256 + 256],
                          start=True, stop=True).then_inc(out_mm, 1)


def kernel(**inputs):
    import numpy as np
    import concourse.bacc as bacc
    from concourse import mybir as _mybir
    from concourse.bass_utils import run_bass_kernel_spmd

    a = {k: np.asarray(v) for k, v in inputs.items()}

    def per_partition(v):
        return v.reshape(-1, 128).T

    def k_major(w):
        return w.reshape(-1, 128, w.shape[1]).transpose(1, 0, 2)

    def twice(w):
        r, c = w.shape
        t = np.zeros((2 * r, 2 * c), w.dtype)
        t[:r, :c] = w
        t[r:, c:] = w
        return t

    b_in = a['L0_gnn_b_in']
    w_in = a['L0_gnn_w_in']
    src, dst = a['src'].astype(np.int32), a['dst'].astype(np.int32)
    y = a['edge_attr_4'].reshape(EC, 128, 4).transpose(1, 0, 2).reshape(128, 4 * EC)
    w2b = np.concatenate([a['L3_gnn_W2'], a['L3_gnn_b2'][None]], 0)
    arrays = {
        'x': a['x'],
        'cols': np.concatenate([per_partition(b_in[:2 * D]), per_partition(b_in[2 * D:]),
                                per_partition(a['L0_gnn_ln1_w']), per_partition(a['L0_gnn_ln1_b']),
                                per_partition(a['L0_gnn_ln2_w']), per_partition(a['L0_gnn_ln2_b']),
                                per_partition(a['L0_gnn_b1']), per_partition(a['L2_gnn_b1']),
                                np.broadcast_to(a['L2_gnn_eps'], (128, 1)), y], 1),
        'idx': np.stack([src.reshape(EC, 128).T, dst.reshape(EC, 128).T], 1),
        'srow': src,
        'feat': np.concatenate([a['edge_attr_8'].reshape(SB, 2, HALF, RB).transpose(1, 3, 0, 2).reshape(2 * RB, SB * HALF),
                                twice(a['L1_gnn_W_mlp1'])], 1),
        'wm23': np.stack([twice(a['L1_gnn_W_mlp2']), twice(a['L1_gnn_W_mlp3'])], 1),
        'w4': np.concatenate([a['L1_gnn_W_mlp4'].reshape(-1, 4, MUL)[:, (1, 0, 2, 3)].reshape(-1, 4 * MUL)] * 2, 0),
        'brow': np.concatenate([a['L0_gnn_b_out'], a['L0_gnn_b2'], a['L2_gnn_b2']]),
        'b31': a['L3_gnn_b1'],
        'wqk': k_major(w_in[:2 * D].T),
        'wv': k_major(w_in[2 * D:].T),
        'wout': k_major(a['L0_gnn_w_out'].T),
        'w1': k_major(a['L0_gnn_w1'].T).reshape(128, DB, 4, 512).transpose(0, 2, 1, 3),
        'w2': k_major(a['L0_gnn_w2'].T),
        'wup': np.stack([a['L1_gnn_W_up0'], a['L1_gnn_W_up1']], 1),
        'wo': np.concatenate([k_major(a['L1_gnn_W_out0']), k_major(a['L1_gnn_W_out1'])], 1),
        'l2w1': k_major(a['L2_gnn_W1']),
        'l2w2': k_major(a['L2_gnn_W2']),
        'l3w1': k_major(a['L3_gnn_W1']),
        'l3w2': w2b,
    }
    arrays = {f"in_{k}": np.ascontiguousarray(v) for k, v in arrays.items()}
    nc = bacc.Bacc("TRN2", target_bir_lowering=False, num_devices=1)
    args = [nc.dram_tensor(k, v.shape, _mybir.dt.from_np(v.dtype), kind="ExternalInput").ap() for k, v in arrays.items()]
    out = nc.dram_tensor("out", (N, D), _mybir.dt.float32, kind="ExternalOutput").ap()
    gnn_stack(nc, *args, out)
    r = run_bass_kernel_spmd(nc, [arrays], core_ids=[0])
    return r.results[0]["out"]
```

```python
import concourse.bass as bass
from concourse import mybir
from contextlib import ExitStack

N = 128
D = 512
DB = D // 128
E = 4096
EC = E // 128
SB = 4
SBC = EC // SB
HALF = 512
H = 8
DH = D // H
F0 = 4 * D
F0B = F0 // 128
F2 = 2 * D
F2B = F2 // 128
F3 = 64
MUL = 128
RB = 8
HID = 64
EPS = 1e-5
NEG = -1e9
SILU_2MOM = 1.679177
AVG_NEIGH = 10.0
T_V, T_SOFT, T_ATTN, T_PROJ, T_NORM2, T_MLP, T_NORM3, T_LIFT = 4, 8, 9, 11, 19, 21, 26, 28
POOL_OH = 10
Y0_POOL = 5
WARM = 12
UNROLL = 4
PATH_SCALE = SILU_2MOM * HID ** -0.5
LAG = 3

C_BQK, C_BV, C_LN1W, C_LN1B, C_LN2W, C_LN2B = 0, 8, 12, 16, 20, 24
C_B1, C_L2B1, C_EPS, C_Y = 28, 44, 52, 53
C_ALL = C_Y + 4 * EC


def gnn_stack(nc, x_d, cols_d, idx_d, srow_d, feat_d, wm23_d, w4_d, brow_d, b31_d,
              wqk_d, wv_d, wout_d, w1_d, w2_d, wup_d, wo_d, l2w1_d, l2w2_d, l3w1_d, l3w2_d, out_d):
    f32, bf16, f32r, i32 = mybir.dt.float32, mybir.dt.bfloat16, mybir.dt.float32r, mybir.dt.int32
    ALU, ACT, AX = mybir.AluOpType, mybir.ActivationFunctionType, mybir.AxisListType

    ctx = ExitStack()
    with ctx:
        base = (nc.sbuf_base + 63) // 64 * 64
        size = {f32: 4, f32r: 4, i32: 4, bf16: 2}

        def at(name, offset, shape, dt):
            return nc.alloc_sbuf_tensor_at(name, shape, dt, offset=offset)

        cursor = [base]

        def sb(name, shape, dt):
            n = size[dt]
            for s in shape[1:]:
                n *= s
            t = at(name, cursor[0], shape, dt)
            cursor[0] += (n + 63) // 64 * 64
            return t

        o_wqk = cursor[0]
        wqk = sb("wqk", [128, DB, 2 * D], f32)
        l2w1 = at("l2w1", o_wqk, [128, DB, F2], f32)
        o_wv = cursor[0]
        wv = sb("wv", [128, DB, D], f32)
        wout = sb("wout", [128, DB, D], f32)
        oh = at("oh", o_wv, [128, EC, 128], f32r)
        o_w1 = cursor[0]
        w1 = sb("w1", [128, 4, DB, 512], f32)
        o_w2 = cursor[0]
        w2 = sb("w2", [128, F0B, D], f32)
        wup = sb("wup", [128, 2, MUL], f32)
        wo = sb("wo", [128, 4, MUL], f32)
        wm23 = sb("wm23", [128, 2, 128], f32)
        w4 = sb("w4", [128, 4 * MUL], f32)
        w4hi = sb("w4hi", [128, 4 * MUL], f32r)
        w4lo = sb("w4lo", [128, 4 * MUL], f32r)
        l3w1 = sb("l3w1", [128, DB, F3], f32)
        l3w2 = sb("l3w2", [F3 + 1, D], f32)
        o_tpw = cursor[0]
        tpw = sb("tpw", [128, EC, 4 * MUL], f32)
        chunk_bytes = 4 * MUL * 4
        stk = [at(f"stk{s}", o_tpw + (26 + 2 * s) * chunk_bytes, [128, 2, HALF], f32r) for s in range(3)]
        stk.append(sb("stk3", [128, 2, HALF], f32r))
        qkT = at("qkT", o_tpw + 20 * chunk_bytes, [128, 8, 128], f32)
        prob = at("prob", o_tpw + 22 * chunk_bytes, [128, H, 128], f32)
        probT = at("probT", o_tpw + 24 * chunk_bytes, [128, H, 128], f32)
        w2_hi = [at(f"w2_hi{i}", o_tpw + (22 + i) * chunk_bytes, [128, D], f32r) for i in range(4)]
        w2_lo = at("w2_lo", o_w2, [128, F0B, D], f32r)
        l2w2 = at("l2w2", o_tpw, [128, F2B, D], f32)
        assert F2B == 8
        msg = at("msg", o_tpw + 8 * chunk_bytes, [128, 4, 128], f32)
        msgT = at("msgT", o_tpw + 10 * chunk_bytes, [128, 8, 128], f32)
        o = o_tpw + 12 * chunk_bytes
        hid2 = [at(f"hid2_{i}", o + i * 512, [128, 128], f32) for i in range(4)]
        hid2_hi = [at(f"hid2_hi{i}", o + (4 + i) * 512, [128, 128], f32r) for i in range(4)]
        hid2_lo = [at(f"hid2_lo{i}", o + (8 + i) * 512, [128, 128], f32r) for i in range(4)]
        l2w2_hi = [at(f"l2w2_hi{i}", o_tpw + (16 + i) * chunk_bytes, [128, D], f32r) for i in range(4)]
        l2w2_lo = at("l2w2_lo", o_tpw, [128, F2B, D], f32r)
        hid0 = [at(f"hid0_{i}", o_wqk + i * 512, [128, 128], f32) for i in range(4)]
        hid0_hi = [at(f"hid0_hi{i}", o_wqk + (4 + i) * 512, [128, 128], f32r) for i in range(4)]
        hid0_lo = [at(f"hid0_lo{i}", o_wqk + (8 + i) * 512, [128, 128], f32r) for i in range(4)]
        assert 4 * 128 * (F0B + EC // 2) <= 4 * DB * 2 * D
        o_src = (o_wqk + 4 * 128 * F0B, o_w1)
        src_i = [at(f"src_i{g}", o_src[g], [128, E // 2], i32) for g in range(2)]
        gsel = [at(f"gsel{g}", o_src[g], [128, EC // 2, 128], f32r) for g in range(2)]
        feat_wm1 = at("feat_wm1", o_w1, [2 * RB, SB * HALF + 128], f32)
        hid = [at(f"hid{i}", o_w1 + 4 * (SB * HALF + 128) + i * 4 * SB * HALF, [128, SB, HALF], f32) for i in range(2)]
        ohs = at("ohs", o_w2, [128, EC, 128], bf16)
        ohd = at("ohd", o_w2 + EC * 256, [128, EC, 128], bf16)
        o = o_w1 + 4 * 128 * (EC // 2)
        ysel = [at(f"ysel{i}", o + i * 1536, [128, 3, 128], f32) for i in range(UNROLL)]
        o += UNROLL * 1536
        tdot = [at(f"tdot{i}", o + i * 512, [128, 128], f32) for i in range(UNROLL)]
        o += UNROLL * 512
        assert o <= o_w2
        xup_hi = at("xup_hi", o_w2, [128, D], f32r)
        xup_lo = at("xup_lo", o_w2 + 2048, [128, D], f32r)
        o = o_w2 + 4096
        prod = [at(f"prod{i}", o + i * 3072, [128, 6, 128], f32) for i in range(UNROLL)]
        o += UNROLL * 3072
        ac_hi = [at(f"ac_hi{i}", o + i * 2048, [128, 512], f32r) for i in range(UNROLL)]
        o += UNROLL * 2048
        ac_lo = [at(f"ac_lo{i}", o + i * 2048, [128, 512], f32r) for i in range(UNROLL)]
        o += UNROLL * 2048
        assert o <= o_w2 + 4 * F0B * D
        warm = sb("warm", [128, D], bf16)
        cols = sb("cols", [128, C_ALL], f32)
        idx_i = sb("idx_i", [128, 2, EC], i32)
        end_f = sb("end_f", [128, 2, EC], f32)
        brow = sb("brow", [128, 3, D], f32)
        b31 = sb("b31", [128, F3], f32)
        ident = sb("ident", [128, 128], f32)
        iota_row = sb("iota_row", [128, 128], f32)
        iota_rb = sb("iota_rb", [128, 128], bf16)
        iota_p = sb("iota_p", [128, 1], f32)
        neghalf = sb("neghalf", [128, 1], f32)
        nscale = sb("nscale", [128, 1], f32)
        cnt_n = sb("cnt_n", [128, 128], f32)
        eps1 = sb("eps1", [128, 1], f32)
        mask = sb("mask", [128, 128], f32)
        adj = sb("adj", [128, 128], f32)
        cnt_sd = sb("cnt_sd", [128, 128], f32)
        cnt_ds = sb("cnt_ds", [128, 128], f32)
        xs = sb("xs", [128, D], f32)
        hn = sb("hn", [128, D], f32)
        zn = sb("zn", [128, D], f32)
        xr = sb("xr", [128, D], f32)
        un = sb("un", [128, D], f32)
        hT = sb("hT", [128, DB, 128], f32)
        y0s = sb("y0s", [128, EC], f32)
        stats = sb("stats", [128, 4, 6], f32)
        mv = sb("mv", [128, 2], f32)
        ve = sb("ve", [128, 1], f32)
        rstd = sb("rstd", [128, 1], f32)
        vn = sb("vn", [128, D], f32)
        smax = sb("smax", [128, H], f32)
        ssum = sb("ssum", [128, H], f32)
        srec = sb("srec", [128, H], f32)
        oT = sb("oT", [128, DB, 128], f32)
        r3 = sb("r3", [128, F3 + 1], f32)
        zT = sb("zT", [F3 + 1, 128], f32)
        assert cursor[0] <= nc.sbuf_usable_end, (cursor[0], nc.sbuf_usable_end)

        P = [ctx.enter_context(nc.psum_tensor(f"bank{i}", [128, 512], f32)) for i in range(8)]

        def sem(name):
            return ctx.enter_context(nc.semaphore(name))

        in_x, in_cols, in_idx, in_feat, in_wm = (sem(f"in_{n}") for n in ("x", "cols", "idx", "feat", "wm"))
        in_srow = [sem(f"in_srow_{g}") for g in range(2)]
        in_w4, in_brow, in_wqk, in_wv, in_wout = (sem(f"in_{n}") for n in ("w4", "brow", "wqk", "wv", "wout"))
        in_small = sem("in_small")
        in_w1 = [sem(f"in_w1_{j}") for j in range(4)]
        in_w2 = [sem(f"in_w2_{j}") for j in range(4)]
        in_l2w1, in_l2w2, out_sent = sem("in_l2w1"), sem("in_l2w2"), sem("out_sent")
        consts_ready, zeroed, idx_cast = sem("consts_ready"), sem("zeroed"), sem("idx_cast")
        warm_ready = sem("warm_ready")
        var_ready, rstd_ready, dve_chain = sem("var_ready"), sem("rstd_ready"), sem("dve_chain")
        h_ready, hT_ready, hT_act, hT_dve = sem("h_ready"), sem("hT_ready"), sem("hT_act"), sem("hT_dve")
        rad_mm, rad_act, split_ready, w4_split = sem("rad_mm"), sem("rad_act"), sem("split_ready"), sem("w4_split")
        hi_ready, tpw_mm, tpw_act, tpw_dve = sem("hi_ready"), sem("tpw_mm"), sem("tpw_act"), sem("tpw_dve")
        onehots_pool = sem("onehots_pool")
        onehots, counts_mm, counts_ready = sem("onehots"), sem("counts_mm"), sem("counts_ready")
        adjT_mm, adjT_ready = sem("adjT_mm"), sem("adjT_ready")
        qk_mm, v_mm, qk_ready, v_ready = sem("qk_mm"), sem("v_mm"), sem("qk_ready"), sem("v_ready")
        scores_mm, max_ready, exp_ready, prob_ready = sem("scores_mm"), sem("max_ready"), sem("exp_ready"), sem("prob_ready")
        probT_mm, probT_act, probT_dve = sem("probT_mm"), sem("probT_act"), sem("probT_dve")
        o_mm, o_ready, proj_mm, hb_ready, xr_ready = (
            sem("o_mm"), sem("o_ready"), sem("proj_mm"), sem("hb_ready"), sem("xr_ready"))
        up_mm, up_act, up_lo, down_step, down_mm, res_ready = (
            sem(n) for n in ("up_mm", "up_act", "up_lo", "down_step", "down_mm", "res_ready"))
        w2_rounded, w2_split = sem("w2_rounded"), sem("w2_split")
        lift_mm, lift_ready = sem("lift_mm"), sem("lift_ready")
        gsel_ready, oh_ready, ysel_ready = sem("gsel_ready"), sem("oh_ready"), sem("ysel_ready")
        y0_in, y0_pool = sem("y0_in"), sem("y0_pool")
        t0_ready, ac_ready, ac_rounded, ac_left = sem("t0_ready"), sem("ac_ready"), sem("ac_rounded"), sem("ac_left")
        gathered, t_steps, prod_ready, scattered = sem("gathered"), sem("t_steps"), sem("prod_ready"), sem("scattered")
        msg_dve, msgT_mm, msgT_dve, msgT_act = (
            sem("msg_dve"), sem("msgT_mm"), sem("msgT_dve"), sem("msgT_act"))
        bd_done, l1_mm, l1_done = sem("bd_done"), sem("l1_mm"), sem("l1_done")
        rst_mm, rst_ready, hb2_ready = sem("rst_mm"), sem("rst_ready"), sem("hb2_ready")
        up2_mm, up2_act, up2_lo, l2w2_rounded, l2w2_split, down2_step, down2_mm = (
            sem(n) for n in ("up2_mm", "up2_act", "up2_lo", "l2w2_rounded", "l2w2_split", "down2_step", "down2_mm"))
        r3_mm, r3_ready, z3_mm, z3_ready, out_mm = (
            sem(n) for n in ("r3_mm", "r3_ready", "z3_mm", "z3_ready", "out_mm"))
        out_ready = [sem(f"out_ready_{g}") for g in range(2)]

        by_dve = (1, 2, 26)
        y0_on_the_way = tuple(c for c in by_dve if c >= T_MLP)
        y0_by_pool = tuple(c for c in range(T_MLP, EC) if c not in by_dve)[:Y0_POOL]
        y0_early, y0_late = (tuple(c for c in cs if c not in by_dve + y0_by_pool)
                             for cs in (range(T_MLP, T_LIFT + 2), range(T_LIFT + 2, EC)))

        def taken(c):
            n = sum(1 for k in by_dve if k <= c)
            return (tpw_dve, n) if c in by_dve else (tpw_act, c + 1 - n)

        def path_views(c):
            return (tpw[:, c, :].rearrange("p (q u) -> p q u", q=4),
                    P[4 + c % 4][:, :].rearrange("p (q u) -> p q u", q=4))

        def y_of(c, m):
            return cols[:, bass.ds(C_Y + 4 * c + m, 1)]

        block = ctx.enter_context(nc.Block())

        @block.sync
        def _(sp):
            sp.dma_start(xs[:, :], x_d).then_inc(in_x, 16)
            sp.dma_start(idx_i[:, :, :], idx_d).then_inc(in_idx, 16)
            sp.dma_start(cols[:, :], cols_d).then_inc(in_cols, 16)
            sp.dma_start(w4[:, :], w4_d).then_inc(in_w4, 16)
            sp.dma_start(wqk[:, :, :], wqk_d).then_inc(in_wqk, 16)
            sp.dma_start(wv[:, :, :], wv_d).then_inc(in_wv, 16)
            sp.dma_start(brow[:, :, :], brow_d.partition_broadcast(128)).then_inc(in_brow, 16)
            sp.dma_start(wout[:, :, :], wout_d).then_inc(in_wout, 16)
            sp.dma_start(wup[:, :, :], wup_d).then_inc(in_small, 16)
            sp.dma_start(wo[:, :, :], wo_d).then_inc(in_small, 16)
            sp.dma_start(l3w1[:, :, :], l3w1_d).then_inc(in_small, 16)
            sp.dma_start(l3w2[:, :], l3w2_d).then_inc(in_small, 16)
            sp.dma_start(b31[:, :], b31_d.partition_broadcast(128)).then_inc(in_small, 16)
            sp.wait_ge(rad_mm, 12)
            sp.wait_ge(split_ready, 2 * SB)
            for j in range(4):
                sp.dma_start(w1[:, j, :, :], w1_d[:, j, :, :]).then_inc(in_w1[j], 16)
            sp.wait_ge(counts_mm, 1)
            for j in range(4):
                sp.dma_start(w2[:, 4 * j:4 * j + 4, :], w2_d[:, 4 * j:4 * j + 4, :]).then_inc(in_w2[j], 16)
            sp.wait_ge(qk_mm, 2)
            sp.dma_start(src_i[0][:, :], srow_d[0:E // 2].partition_broadcast(128)).then_inc(in_srow[0], 16)
            sp.wait_ge(up_mm, F0B)
            sp.dma_start(src_i[1][:, :], srow_d[E // 2:E].partition_broadcast(128)).then_inc(in_srow[1], 16)
            sp.wait_ge(down_mm, 2)
            sp.wait_ge(gathered, EC // 2)
            sp.dma_start(l2w1[:, :, :], l2w1_d).then_inc(in_l2w1, 16)
            sp.wait_ge(prod_ready, F2B)
            sp.dma_start(l2w2[:, :, :], l2w2_d).then_inc(in_l2w2, 16)
            for g in range(2):
                half = slice(g * 256, g * 256 + 256)
                sp.wait_ge(out_ready[g], 1)
                sp.dma_start(out_d[:, half], un[:, half]).then_inc(out_sent, 16)
            sp.wait_ge(out_sent, 32)

        @block.gpsimd
        def _(pool):
            pool.memset(neghalf[:, :], -0.5).then_inc(consts_ready, 1)
            pool.iota(iota_row[:, :], pattern=[[1, 128]], base=0, channel_multiplier=0,
                      allow_small_or_imprecise_dtypes=True).then_inc(consts_ready, 1)
            pool.iota(iota_p[:, :], pattern=[[1, 1]], base=0, channel_multiplier=1,
                      allow_small_or_imprecise_dtypes=True).then_inc(consts_ready, 1)
            pool.memset(ident[:, :], 0.0).then_inc(zeroed, 1)
            pool.wait_ge(zeroed, 1)
            pool.affine_select(out=ident[:, :], in_=ident[:, :], compare_op=ALU.not_equal, fill=1.0,
                               base=0, pattern=[[-1, 128]], channel_multiplier=1).then_inc(consts_ready, 1)

            def root(n):
                pool.wait_ge(var_ready, n)
                pool.tensor_tensor(rstd[:, :], ve[:, :], neghalf[:, :], ALU.pow).then_inc(rstd_ready, 1)

            pool.wait_ge(consts_ready, 4)
            root(1)
            root(2)
            pool.wait_ge(idx_cast, 1)
            for c in range(EC - POOL_OH, EC):
                pool.tensor_scalar(ohd[:, c, :], iota_row[:, :], end_f[:, 1, c:c + 1], None,
                                   ALU.is_equal).then_inc(onehots_pool, 1)
            pool.wait_ge(h_ready, 1)
            pool.wait_ge(in_brow, 16)
            pool.tensor_tensor(un[:, :], hn[:, :], brow[:, 0, :], ALU.add).then_inc(hb_ready, 1)
            pool.tensor_tensor(xs[:, :], xs[:, :], brow[:, 1, :], ALU.add).then_inc(hb_ready, 1)
            root(3)
            pool.wait_ge(xr_ready, 1)
            pool.wait_ge(hb_ready, 2)
            pool.tensor_tensor(xs[:, :], xs[:, :], xr[:, :], ALU.add).then_inc(hb_ready, 1)
            pool.wait_ge(proj_mm, 1)
            for c in range(EC):
                pool.tensor_scalar(oh[:, c, :], iota_row[:, :], end_f[:, 1, c:c + 1], None,
                                   ALU.is_equal).then_inc(oh_ready, 1)

            def select(c):
                g, i = divmod(c, EC // 2)
                pool.tensor_scalar(gsel[g][:, i, :], src_i[g][:, i * 128:(i + 1) * 128], iota_p[:, :], None,
                                   ALU.is_equal).then_inc(gsel_ready, 1)

            pool.wait_ge(in_srow[0], 16)
            for c in range(EC // 2):
                select(c)
            root(4)
            for c in y0_by_pool:
                pool.wait_ge(*taken(c))
                pool.tensor_scalar(tpw[:, c, 128:384], tpw[:, c, 128:384], cols[:, C_Y + 4 * c:C_Y + 4 * c + 1], None,
                                   ALU.mult).then_inc(y0_pool, 1)
            pool.wait_ge(in_srow[1], 16)
            for c in range(EC):
                b = c % UNROLL
                pool.wait_ge(ac_rounded, c + 1)
                pool.tensor_tensor(ac_lo[b][:, :], prod[b][:, 1:5, :].rearrange("p q u -> p (q u)"), ac_hi[b][:, :],
                                   ALU.subtract).then_inc(ac_left, 1)
                if c % 3 < 2 and EC // 2 + c // 3 * 2 + c % 3 < EC:
                    select(EC // 2 + c // 3 * 2 + c % 3)
            root(5)
            pool.wait_ge(h_ready, 5)
            pool.tensor_tensor(xs[:, :], xs[:, :], brow[:, 2, :], ALU.add).then_inc(hb2_ready, 1)
            pool.wait_ge(rstd_ready, 5)
            pool.tensor_scalar(un[:, :], hn[:, :], rstd[:, :], None, ALU.mult).then_inc(hb2_ready, 1)
            pool.wait_ge(hb2_ready, 2)
            pool.tensor_tensor(xs[:, :], xs[:, :], un[:, :], ALU.add).then_inc(hb2_ready, 1)
            root(6)

        @block.scalar
        def _(act):
            act.dma_start(feat_wm1[:, :], feat_d).then_inc(in_feat, 16)
            act.dma_start(wm23[:, :, :], wm23_d).then_inc(in_wm, 16)
            act.preload_act_table(ACT.Silu)

            def radial(layer):
                for s in range(SB):
                    act.wait_ge(rad_mm, SB * layer + s + 1)
                    scale = RB ** -0.5 if layer == 0 else SILU_2MOM * HID ** -0.5
                    act.activation(hid[layer % 2][:, s, :], P[4 + s][:, :], ACT.Silu,
                                   scale=scale).then_inc(rad_act, 1)

            def tpw_out(cs):
                for c in cs:
                    if c not in by_dve:
                        act.wait_ge(tpw_mm, c + 1)
                        act.activation(tpw[:, c, :], P[4 + c % 4][:, :], ACT.Copy,
                                       scale=PATH_SCALE).then_inc(tpw_act, 1)

            def xn_out(w, b):
                for j in (2, 3):
                    act.activation(hT[:, j, :], P[1][:, (j - 2) * 128:(j - 1) * 128], ACT.Identity,
                                   scale=cols[:, w + j:w + j + 1],
                                   bias=cols[:, b + j:b + j + 1]).then_inc(hT_act, 1)

            radial(0)
            act.wait_ge(in_cols, 16)
            act.wait_ge(hT_ready, 1)
            xn_out(C_LN1W, C_LN1B)
            radial(1)
            radial(2)
            act.wait_ge(rad_act, 3 * SB)
            for s in range(SB):
                act.activation(stk[s][0:64, 0, :], hid[0][0:64, s, :], ACT.Copy).then_inc(hi_ready, 1)
                act.activation(stk[s][64:128, 1, :], hid[0][64:128, s, :], ACT.Copy).then_inc(hi_ready, 1)
            act.preload_act_table(ACT.Exp)
            tpw_out(range(0, 1))
            for g in range(2):
                act.wait_ge(max_ready, g + 1)
                for b in range(4):
                    s = 4 * g + b
                    act.activation(prob[:, s, :], prob[:, s, :], ACT.Exp, bias=smax[:, s:s + 1],
                                   accum_out=ssum[:, s:s + 1]).then_inc(exp_ready, 1)
            act.wait_ge(v_mm, 1)
            act.activation(vn[:, :], P[0][:, :], ACT.Copy).then_inc(v_ready, 1)
            tpw_out(range(1, T_SOFT))
            act.wait_ge(probT_mm, 2)
            act.activation(probT[:, 4:8, :], P[1][:, :], ACT.Copy).then_inc(probT_act, 1)
            tpw_out(range(T_SOFT, T_NORM2 - 2))
            act.wait_ge(hT_ready, 2)
            xn_out(C_LN2W, C_LN2B)
            tpw_out(range(T_NORM2 - 2, T_MLP))
            for j in range(F0B):
                act.wait_ge(up_mm, j + 1)
                if j >= 4:
                    act.wait_ge(up_lo, j - 3)
                    act.wait_ge(down_step, j - 3)
                for h in (hid0, hid0_hi):
                    last = act.activation(h[j % 4][:, :], P[j % 3][:, 0:128], ACT.Relu,
                                          bias=cols[:, C_B1 + j:C_B1 + j + 1])
                last.then_inc(up_act, 1)
                n = j + 2
                if n < F0B:
                    act.wait_ge(in_w2[n // 4], 16)
                    if n >= 4:
                        act.wait_ge(down_step, n - 3)
                        act.wait_ge(w2_split, n - 3)
                    act.activation(w2_hi[n % 4][:, :], w2[:, n, :], ACT.Copy).then_inc(w2_rounded, 1)
            tpw_out(range(T_MLP, T_NORM3))
            act.wait_ge(hT_ready, 3)
            act.activation(hT[:, 2:4, :], P[1][:, 0:256], ACT.Copy).then_inc(hT_act, 1)

            def first_product(c, k):
                act.wait_ge(gathered, c + 1)
                act.activation(tdot[k][:, :], P[k][:, 128:256], ACT.Copy, scale=y_of(c, 1)).then_inc(t0_ready, 1)

            def weigh(c, k, first):
                if not first:
                    act.wait_ge(scattered, c - UNROLL + 1)
                one = oh[:, bass.ds(c, 1), :].rearrange("p a n -> p (a n)").bitcast(f32)
                for m in range(3):
                    last = act.activation(ysel[k][:, m, :], one, ACT.Copy, scale=y_of(c, m + 1))
                last.then_inc(ysel_ready, 1)

            def rounded(c, k):
                act.wait_ge(ac_ready, c + 1)
                act.activation(ac_hi[k][:, :], prod[k][:, 1:5, :].rearrange("p q u -> p (q u)"),
                               ACT.Copy).then_inc(ac_rounded, 1)

            act.wait_ge(oh_ready, EC)
            weigh(0, 0, True)
            tpw_out(range(T_NORM3, EC))
            first_product(0, 0)
            weigh(1, 1, True)
            first_product(1, 1)
            for k in range(2, UNROLL):
                rounded(k - 2, k - 2)
                first_product(k, k)
                weigh(k, k, True)
            rounded(UNROLL - 2, UNROLL - 2)
            with act.Fori(1, EC // UNROLL) as i:
                for k in range(UNROLL):
                    first_product(i * UNROLL + k, k)
                    weigh(i * UNROLL + k, k, False)
                    rounded(i * UNROLL + (k - 1), (k - 1) % UNROLL)
            rounded(EC - 1, UNROLL - 1)
            act.wait_ge(bd_done, 1)
            act.activation(msgT[:, 4:7, :], P[7][:, 0:384], ACT.Copy).then_inc(msgT_act, 1)
            act.activation(msgT[:, 7, :], P[7][:, 384:512], ACT.Copy, scale=3.0 ** -0.5).then_inc(msgT_act, 1)
            act.wait_ge(rst_mm, 2)
            act.activation(hT[:, 2:4, :], P[1][:, 0:256], ACT.Copy).then_inc(rst_ready, 1)
            act.wait_ge(adjT_mm, 1)
            act.activation(cnt_ds[:, :], P[7][:, 0:128], ACT.Copy).then_inc(adjT_ready, 1)
            act.wait_ge(in_l2w2, 16)
            for j in range(F2B):
                act.wait_ge(up2_mm, j + 1)
                if j >= 4:
                    act.wait_ge(up2_lo, j - 3)
                    act.wait_ge(down2_step, j - 3)
                for h in (hid2, hid2_hi):
                    last = act.activation(h[j % 4][:, :], P[(1, 2, 4, 5)[j % 4]][:, 0:128], ACT.Relu,
                                          bias=cols[:, C_L2B1 + j:C_L2B1 + j + 1])
                last.then_inc(up2_act, 1)
                n = j + 2
                if n < F2B:
                    if n >= 4:
                        act.wait_ge(down2_step, n - 3)
                        act.wait_ge(l2w2_split, n - 3)
                    act.activation(l2w2_hi[n % 4][:, :], l2w2[:, n, :], ACT.Copy).then_inc(l2w2_rounded, 1)
            act.wait_ge(hT_ready, 4)
            act.activation(hT[:, 2:4, :], P[1][:, 0:256], ACT.Copy).then_inc(hT_act, 1)
            act.wait_ge(out_mm, 2)
            act.activation(un[:, 256:512], P[6][:, 0:256], ACT.Copy).then_inc(out_ready[1], 1)

        @block.vector
        def _(dve):
            chained = [0]

            def link(ins):
                chained[0] += 1
                ins.then_inc(dve_chain, 1)
                dve.wait_ge(dve_chain, chained[0])

            def stat(parts):
                link(dve.bn_aggr(mv[:, :], stats[:, 0:parts, :].rearrange("p n s -> p (n s)")))
                dve.tensor_scalar(ve[:, :], mv[:, 1:2], EPS, None, ALU.add).then_inc(var_ready, 1)

            def relu_norm(n):
                link(dve.bn_stats(stats[:, 0, :], xs[:, :]))
                stat(1)
                link(dve.tensor_scalar(hn[:, :], xs[:, :], mv[:, 0:1], 0.0, ALU.subtract, ALU.max))
                dve.wait_ge(rstd_ready, n)
                ins = dve.tensor_scalar(hn[:, :], hn[:, :], rstd[:, :], None, ALU.mult)
                ins.then_inc(h_ready, 1)

            def relu_center(parts):
                stat(parts)
                dve.tensor_scalar(hn[:, :], xs[:, :], mv[:, 0:1], 0.0, ALU.subtract, ALU.max).then_inc(h_ready, 1)

            def residual(bank_a, bank_b, made, before):
                for g in range(2):
                    half = slice(g * 256, g * 256 + 256)
                    dve.wait_ge(made, g + 1)
                    dve.tensor_tensor(xs[:, half], P[(bank_a, bank_b)[g]][:, 0:256], xs[:, half],
                                      ALU.add).then_inc(res_ready, 1)
                for g in range(2):
                    dve.wait_ge(res_ready, before + g + 1)
                    dve.bn_stats(stats[:, g, :], xs[:, g * 256:g * 256 + 256]).then_inc(dve_chain, 1)
                chained[0] += 2
                dve.wait_ge(dve_chain, chained[0])

            def affine_norm(src, n):
                link(dve.bn_stats(stats[:, 0, :], src))
                stat(1)
                dve.wait_ge(rstd_ready, n)
                dve.tensor_scalar(zn[:, :], src, mv[:, 0:1], rstd[:, :], ALU.subtract, ALU.mult)\
                   .then_inc(h_ready, 1)

            def tpw_out(cs):
                for c in cs:
                    if c not in by_dve:
                        continue
                    dve.wait_ge(tpw_mm, c + 1)
                    if c < T_MLP:
                        dve.tensor_scalar(tpw[:, c, :], P[4 + c % 4][:, :], PATH_SCALE, None,
                                          ALU.mult).then_inc(tpw_dve, 1)
                    else:
                        w, q = path_views(c)
                        dve.tensor_scalar(w[:, 1:3, :], q[:, 1:3, :], y0s[:, c:c + 1], None, ALU.mult)
                        dve.tensor_scalar(w[:, 0:4:3, :], q[:, 0:4:3, :], PATH_SCALE, None, ALU.mult).then_inc(tpw_dve, 1)

            def times_y0(c):
                dve.wait_ge(*taken(c))
                dve.tensor_scalar(tpw[:, c, 128:384], tpw[:, c, 128:384], cols[:, C_Y + 4 * c:C_Y + 4 * c + 1], None,
                                  ALU.mult).then_inc(y0_in, 1)

            dve.memset(warm[:, :], 0.0).then_inc(warm_ready, 1)
            dve.wait_ge(in_x, 16)
            relu_norm(1)
            dve.wait_ge(h_ready, 1)
            affine_norm(hn[:, :], 2)
            dve.wait_ge(consts_ready, 4)
            link(dve.tensor_copy(iota_rb[:, :], iota_row[:, :]))
            dve.wait_ge(in_idx, 16)
            dve.tensor_copy(end_f[:, :, :], idx_i[:, :, :]).then_inc(idx_cast, 1)
            dve.wait_ge(idx_cast, 1)

            def onehot(k, t, cs):
                for c in cs:
                    dve.tensor_scalar(t[:, c, :], iota_rb[:, :], end_f[:, k, c:c + 1], None,
                                      ALU.is_equal).then_inc(onehots, 1)

            onehot(0, ohs, range(12))
            dve.wait_ge(in_cols, 16)
            dve.wait_ge(hT_ready, 1)
            for j in (0, 1):
                dve.tensor_scalar(hT[:, j, :], P[0][:, j * 128:(j + 1) * 128],
                                  cols[:, C_LN1W + j:C_LN1W + j + 1], cols[:, C_LN1B + j:C_LN1B + j + 1],
                                  ALU.mult, ALU.add).then_inc(hT_dve, 1)
            link(dve.tensor_scalar(y0s[:, :], cols[:, C_Y:C_Y + 4 * EC:4], PATH_SCALE, None, ALU.mult))
            dve.wait_ge(in_w4, 16)
            link(dve.tensor_copy(w4hi[:, :], w4[:, :]))
            dve.tensor_tensor(w4lo[:, :], w4[:, :], w4hi[:, :], ALU.subtract).then_inc(w4_split, 1)
            onehot(0, ohs, range(12, EC))
            onehot(1, ohd, range(EC - POOL_OH))
            for s in range(SB):
                h = hid[0][:, s, :]
                dve.wait_ge(hi_ready, 2 * s + 1)
                dve.tensor_tensor(stk[s][64:128, 0, :], h[0:64, :], stk[s][0:64, 0, :],
                                  ALU.subtract).then_inc(split_ready, 1)
                dve.wait_ge(hi_ready, 2 * s + 2)
                dve.tensor_tensor(stk[s][0:64, 1, :], h[64:128, :], stk[s][64:128, 1, :],
                                  ALU.subtract).then_inc(split_ready, 1)
            for g in range(2):
                dve.wait_ge(qk_mm, g + 1)
                dve.tensor_tensor(qkT[:, 4 * g:4 * g + 4, :],
                                  P[2 + g][:, :].rearrange("p (b n) -> p b n", b=4),
                                  cols[:, C_BQK + 4 * g:C_BQK + 4 * g + 4].unsqueeze(2).broadcast_to([128, 4, 128]),
                                  ALU.add).then_inc(qk_ready, 1)
            dve.wait_ge(counts_mm, 1)
            link(dve.tensor_tensor(adj[:, :], P[1][:, 0:128], ident[:, :], ALU.add))
            dve.tensor_scalar(eps1[:, :], cols[:, C_EPS:C_EPS + 1], 1.0, None, ALU.add).then_inc(dve_chain, 1)
            link(dve.tensor_scalar(mask[:, :], adj[:, :], 0.5, NEG, ALU.is_lt, ALU.mult))
            chained[0] += 1
            dve.wait_ge(dve_chain, chained[0])
            dve.scalar_tensor_tensor(out=cnt_sd[:, :], in0=ident[:, :], scalar=eps1[:, :], in1=P[1][:, 0:128],
                                     op0=ALU.mult, op1=ALU.add).then_inc(counts_ready, 1)
            for g in range(2):
                dve.wait_ge(scores_mm, g + 1)
                link(dve.scalar_tensor_tensor(out=prob[:, 4 * g:4 * g + 4, :],
                                              in0=P[2 + g][:, :].rearrange("p (b n) -> p b n", b=4),
                                              scalar=DH ** -0.5,
                                              in1=mask[:, :].unsqueeze(1).broadcast_to([128, 4, 128]),
                                              op0=ALU.mult, op1=ALU.add))
                link(dve.tensor_reduce(smax[:, 4 * g:4 * g + 4], prob[:, 4 * g:4 * g + 4, :], AX.X, ALU.max))
                dve.tensor_scalar(smax[:, 4 * g:4 * g + 4], smax[:, 4 * g:4 * g + 4], -1.0, None,
                                  ALU.mult).then_inc(max_ready, 1)
            tpw_out(range(0, T_SOFT))
            for g in range(2):
                dve.wait_ge(exp_ready, 4 * g + 4)
                link(dve.reciprocal(srec[:, 4 * g:4 * g + 4], ssum[:, 4 * g:4 * g + 4]))
                for b in range(4):
                    s = 4 * g + b
                    dve.tensor_scalar(prob[:, s, :], prob[:, s, :], srec[:, s:s + 1], None,
                                      ALU.mult).then_inc(prob_ready, 1)
            dve.wait_ge(probT_mm, 1)
            dve.tensor_copy(probT[:, 0:4, :], P[0][:, :].rearrange("p (b n) -> p b n", b=4)).then_inc(probT_dve, 1)
            tpw_out(range(T_SOFT, T_ATTN))
            dve.wait_ge(o_mm, 1)
            dve.tensor_tensor(oT[:, :, :], P[2][:, :].rearrange("p (b n) -> p b n", b=4),
                              cols[:, C_BV:C_BV + 4].unsqueeze(2).broadcast_to([128, 4, 128]),
                              ALU.add).then_inc(o_ready, 1)
            tpw_out(range(T_ATTN, T_PROJ))
            dve.wait_ge(proj_mm, 1)
            dve.wait_ge(hb_ready, 1)
            dve.tensor_tensor(xr[:, :], P[3][:, :], un[:, :], ALU.add).then_inc(xr_ready, 1)
            dve.wait_ge(xr_ready, 1)
            affine_norm(xr[:, :], 3)

            def split_w2(j):
                dve.tensor_tensor(w2_lo[:, j, :], w2[:, j, :], w2_hi[j % 4][:, :], ALU.subtract).then_inc(w2_split, 1)

            for j in range(2):
                if j == 1:
                    dve.wait_ge(hT_ready, 2)
                    for b in (0, 1):
                        dve.tensor_scalar(hT[:, b, :], P[0][:, b * 128:(b + 1) * 128],
                                          cols[:, C_LN2W + b:C_LN2W + b + 1], cols[:, C_LN2B + b:C_LN2B + b + 1],
                                          ALU.mult, ALU.add).then_inc(hT_dve, 1)
                dve.wait_ge(in_w2[0], 16)
                link(dve.tensor_copy(w2_hi[j][:, :], w2[:, j, :]))
                split_w2(j)
            tpw_out(range(T_PROJ, T_MLP))
            for j in range(F0B):
                dve.wait_ge(up_act, j + 1)
                if j >= 4:
                    dve.wait_ge(down_step, j - 3)
                dve.tensor_tensor(hid0_lo[j % 4][:, :], hid0[j % 4][:, :], hid0_hi[j % 4][:, :],
                                  ALU.subtract).then_inc(up_lo, 1)
                if j + 2 < F0B:
                    dve.wait_ge(w2_rounded, j + 1)
                    split_w2(j + 2)
                for c in range(j * T_MLP // F0B, (j + 1) * T_MLP // F0B):
                    times_y0(c)
            dve.wait_ge(hb_ready, 3)
            residual(3, 4, down_mm, 0)

            relu_center(2)
            dve.wait_ge(hT_ready, 3)
            dve.tensor_copy(hT[:, 0:2, :], P[0][:, 0:256].rearrange("p (b n) -> p b n", b=2)).then_inc(hT_dve, 1)
            dve.wait_ge(rstd_ready, 4)
            link(dve.tensor_scalar(nscale[:, :], rstd[:, :], MUL ** -0.5, None, ALU.mult))
            tpw_out(range(T_MLP, T_LIFT))
            dve.wait_ge(lift_mm, 1)
            link(dve.tensor_scalar(xup_hi[:, :], P[2][:, :], nscale[:, :], None, ALU.mult))
            dve.scalar_tensor_tensor(out=xup_lo[:, :], in0=P[2][:, :], scalar=nscale[:, :], in1=xup_hi[:, :],
                                     op0=ALU.mult, op1=ALU.subtract).then_inc(lift_ready, 1)

            def messages(c, k, first):
                g, p, t = P[k], prod[k], tdot[k]
                w = tpw[:, bass.ds(c, 1), :].rearrange("p a (q u) -> p (a q) u", q=4)
                dve.wait_ge(t0_ready, c + 1)
                if not first:
                    dve.wait_ge(scattered, c - UNROLL + 1)
                dve.scalar_tensor_tensor(out=t[:, :], in0=g[:, 256:384], scalar=y_of(c, 2), in1=t[:, :],
                                         op0=ALU.mult, op1=ALU.add).then_inc(t_steps, 1)
                dve.tensor_tensor(p[:, 0:2, :], g[:, 0:128].unsqueeze(1).broadcast_to([128, 2, 128]),
                                  w[:, 0:2, :], ALU.mult)
                dve.wait_ge(t_steps, 2 * c + 1)
                dve.scalar_tensor_tensor(out=t[:, :], in0=g[:, 384:512], scalar=y_of(c, 3), in1=t[:, :],
                                         op0=ALU.mult, op1=ALU.add).then_inc(t_steps, 1)
                dve.tensor_tensor(p[:, 2:5, :], g[:, 128:512].rearrange("p (m u) -> p m u", m=3),
                                  w[:, 2:3, :].broadcast_to([128, 3, 128]), ALU.mult).then_inc(ac_ready, 1)
                dve.wait_ge(t_steps, 2 * c + 2)
                dve.tensor_tensor(p[:, 5, :], t[:, :], w[:, 3, :], ALU.mult).then_inc(prod_ready, 1)

            for c in y0_early:
                times_y0(c)
            dve.wait_ge(y0_in, UNROLL)
            for k in range(UNROLL):
                messages(k, k, True)
            for c in y0_late:
                times_y0(c)
            dve.wait_ge(tpw_dve, len(by_dve))
            dve.wait_ge(y0_in, EC - len(y0_by_pool) - len(y0_on_the_way))
            dve.wait_ge(y0_pool, len(y0_by_pool))
            with dve.Fori(1, EC // UNROLL) as i:
                for k in range(UNROLL):
                    messages(i * UNROLL + k, k, False)
            dve.wait_ge(scattered, EC)
            for g in range(2):
                dve.tensor_copy(msg[:, 2 * g:2 * g + 2, :],
                                P[6][:, 256 * g:256 * g + 256].rearrange("p (b n) -> p b n", b=2)).then_inc(msg_dve, 1)
            dve.wait_ge(msgT_mm, 1)
            dve.tensor_copy(msgT[:, 0:4, :], P[0][:, :].rearrange("p (b n) -> p b n", b=4)).then_inc(msgT_dve, 1)
            final = (2 * MUL) ** -0.5 / AVG_NEIGH
            plane = [xs[:, 0:128]] + [xs[:, 128 + m:512:3] for m in range(3)]
            for n in range(5):
                if n < 4:
                    dve.wait_ge(l1_mm, n + 1)
                    dve.scalar_tensor_tensor(out=plane[n], in0=P[2 + n][:, 0:128], scalar=final, in1=plane[n],
                                             op0=ALU.mult, op1=ALU.add).then_inc(l1_done, 1)
                if n >= 1:
                    dve.wait_ge(l1_done, n)
                    dve.bn_stats(stats[:, n - 1, :], plane[n - 1]).then_inc(dve_chain, 1)
            chained[0] += 4
            dve.wait_ge(dve_chain, chained[0])

            relu_center(4)
            dve.wait_ge(rstd_ready, 5)
            dve.tensor_scalar(cnt_n[:, :], cnt_sd[:, :], rstd[:, :], None, ALU.mult).then_inc(h_ready, 1)
            dve.wait_ge(rst_mm, 1)
            dve.tensor_copy(hT[:, 0:2, :], P[0][:, 0:256].rearrange("p (b n) -> p b n", b=2)).then_inc(rst_ready, 1)

            def split_l2w2(j):
                dve.tensor_tensor(l2w2_lo[:, j, :], l2w2[:, j, :], l2w2_hi[j % 4][:, :],
                                  ALU.subtract).then_inc(l2w2_split, 1)

            dve.wait_ge(in_l2w2, 16)
            for j in range(2):
                link(dve.tensor_copy(l2w2_hi[j][:, :], l2w2[:, j, :]))
                split_l2w2(j)
            for j in range(F2B):
                dve.wait_ge(up2_act, j + 1)
                if j >= 4:
                    dve.wait_ge(down2_step, j - 3)
                dve.tensor_tensor(hid2_lo[j % 4][:, :], hid2[j % 4][:, :], hid2_hi[j % 4][:, :],
                                  ALU.subtract).then_inc(up2_lo, 1)
                if j + 2 < F2B:
                    dve.wait_ge(l2w2_rounded, j + 1)
                    split_l2w2(j + 2)
            dve.wait_ge(hb2_ready, 3)
            residual(3, 6, down2_mm, 2)

            relu_center(2)
            dve.memset(r3[:, F3:F3 + 1], 1.0).then_inc(r3_ready, 1)
            dve.wait_ge(hT_ready, 4)
            dve.tensor_copy(hT[:, 0:2, :], P[0][:, 0:256].rearrange("p (b n) -> p b n", b=2)).then_inc(hT_dve, 1)
            dve.wait_ge(rstd_ready, 6)
            dve.wait_ge(r3_mm, 1)
            link(dve.scalar_tensor_tensor(out=r3[:, 0:F3], in0=P[2][:, 0:F3], scalar=rstd[:, :], in1=b31[:, :],
                                          op0=ALU.mult, op1=ALU.add))
            dve.tensor_scalar(r3[:, 0:F3], r3[:, 0:F3], 0.0, None, ALU.max).then_inc(r3_ready, 1)
            dve.wait_ge(z3_mm, 1)
            dve.tensor_copy(zT[:, :], P[4][0:F3 + 1, 0:128]).then_inc(z3_ready, 1)
            dve.wait_ge(out_mm, 1)
            dve.tensor_copy(un[:, 0:256], P[5][:, 0:256]).then_inc(out_ready[0], 1)

        @block.tensor
        def _(pe):
            def transposes(src, n, dsts, signal):
                for j in range(n):
                    last = pe.transpose(dsts[j], src[j], ident[:, :])
                last.then_inc(signal, 1)

            def radial(layer):
                for s in range(SB):
                    if layer == 0:
                        pe.matmul(P[4 + s][:, :], feat_wm1[:, SB * HALF:], feat_wm1[:, s * HALF:(s + 1) * HALF],
                                  start=True, stop=True).then_inc(rad_mm, 1)
                    else:
                        pe.wait_ge(rad_act, SB * (layer - 1) + s + 1)
                        pe.matmul(P[4 + s][:, :], wm23[:, layer - 1, :], hid[(layer - 1) % 2][:, s, :],
                                  start=True, stop=True).then_inc(rad_mm, 1)

            def paths(cs):
                for c in cs:
                    s, half, col = c // SBC, c % SBC // 4, c % 4 * 128
                    if c >= 4:
                        pe.wait_ge(*taken(c - 4))
                    if c == -(-T_MLP // 4) * 4:
                        pe.wait_ge(res_ready, 2)
                    h = stk[s][:, half, col:col + 128]
                    pe.matmul(P[4 + c % 4][:, :], h, w4hi[:, :], start=True, stop=False)
                    pe.matmul(P[4 + c % 4][:, :], h, w4lo[:, :], start=False, stop=True).then_inc(tpw_mm, 1)

            def keep_clock(n):
                for _ in range(n):
                    pe.matmul(P[7][:, :], warm[:, 0:128], warm[:, :], start=True, stop=True)

            def blocks(src):
                return [src[:, j * 128:(j + 1) * 128] for j in range(4)]

            two_banks = [P[j // 2][:, (j % 2) * 128:(j % 2 + 1) * 128] for j in range(4)]

            pe.wait_ge(warm_ready, 1)
            for _ in range(WARM):
                pe.matmul(P[0][:, :], warm[:, 0:128], warm[:, :], start=True, stop=True)
            pe.wait_ge(in_feat, 16)
            radial(0)
            pe.wait_ge(consts_ready, 4)
            pe.wait_ge(h_ready, 2)
            transposes(blocks(zn), 4, two_banks, hT_ready)
            pe.wait_ge(in_wm, 16)
            radial(1)
            radial(2)
            pe.wait_ge(in_wqk, 16)
            pe.wait_ge(hT_act, 2)
            pe.wait_ge(hT_dve, 2)
            for b in range(8):
                for j in range(DB):
                    last = pe.matmul(P[2 + b // 4][:, b % 4 * 128:(b % 4 + 1) * 128], wqk[:, j, b * 128:(b + 1) * 128],
                                     hT[:, j, :], start=j == 0, stop=j == DB - 1)
                if b % 4 == 3:
                    last.then_inc(qk_mm, 1)
            pe.wait_ge(onehots, 2 * EC - POOL_OH)
            pe.wait_ge(onehots_pool, POOL_OH)
            for c in range(EC):
                last = pe.matmul(P[1][:, 0:128], ohs[:, c, :], ohd[:, c, :], start=c == 0, stop=c == EC - 1)
            last.then_inc(counts_mm, 1)
            pe.wait_ge(qk_ready, 2)
            for g in range(2):
                rows = slice(64 * g, 64 * g + 64)
                for b in range(4):
                    last = pe.matmul(P[2 + g][:, b * 128:(b + 1) * 128], qkT[rows, b, :], qkT[rows, 4 + b, :],
                                     start=True, stop=True)
                last.then_inc(scores_mm, 1)
            pe.wait_ge(w4_split, 1)
            pe.wait_ge(split_ready, 2 * SB)
            paths(range(0, T_V))
            pe.wait_ge(in_wv, 16)
            for j in range(DB):
                last = pe.matmul(P[0][:, :], hT[:, j, :], wv[:, j, :], start=j == 0, stop=j == DB - 1)
            last.then_inc(v_mm, 1)
            paths(range(T_V, T_SOFT))
            pe.wait_ge(v_ready, 1)
            pe.wait_ge(counts_ready, 1)
            for g in range(2):
                for b in range(4):
                    pe.wait_ge(prob_ready, 4 * g + b + 1)
                    last = pe.transpose(P[g][:, b * 128:(b + 1) * 128], prob[:, 4 * g + b, :], ident[:, :])
                last.then_inc(probT_mm, 1)
            paths(range(T_SOFT, T_ATTN))
            for g in range(2):
                if g == 0:
                    pe.wait_ge(probT_dve, 1)
                else:
                    pe.wait_ge(probT_act, 1)
                for b in range(4):
                    h = 2 * b + g
                    last = pe.matmul(P[2][64 * g:64 * g + 64, b * 128:(b + 1) * 128], vn[:, h * DH:(h + 1) * DH],
                                     probT[:, 4 * g + b, :], start=True, stop=True)
            last.then_inc(o_mm, 1)
            paths(range(T_ATTN, T_PROJ))
            pe.wait_ge(o_ready, 1)
            pe.wait_ge(in_wout, 16)
            for j in range(DB):
                last = pe.matmul(P[3][:, :], oT[:, j, :], wout[:, j, :], start=j == 0, stop=j == DB - 1)
            last.then_inc(proj_mm, 1)
            paths(range(T_PROJ, T_NORM2))
            pe.wait_ge(h_ready, 3)
            transposes(blocks(zn), 4, two_banks, hT_ready)
            paths(range(T_NORM2, T_MLP))
            pe.wait_ge(hT_act, 4)
            pe.wait_ge(hT_dve, 4)

            def down_block(j, n, h_hi, h_lo, w_hi, w_lo, banks, step, done):
                hi, lo = h_hi[j % 4][:, :], h_lo[j % 4][:, :]
                for g in range(2):
                    half = slice(g * 256, g * 256 + 256)
                    out = P[banks[g]][:, 0:256]
                    pe.matmul(out, lo, w_hi[j % 4][:, half], start=j == 0, stop=False)
                    pe.matmul(out, hi, w_lo[:, j, half], start=False, stop=False)
                    last = pe.matmul(out, hi, w_hi[j % 4][:, half], start=False, stop=j == n - 1)
                    if j == n - 1:
                        last.then_inc(done, 1)
                if j < n - 1:
                    last.then_inc(step, 1)

            def down(j):
                pe.wait_ge(up_lo, j + 1)
                pe.wait_ge(w2_split, j + 1)
                down_block(j, F0B, hid0_hi, hid0_lo, w2_hi, w2_lo, (3, 4), down_step, down_mm)

            for f in range(F0B):
                if f % 4 == 0:
                    pe.wait_ge(in_w1[f // 4], 16)
                for j in range(DB):
                    last = pe.matmul(P[f % 3][:, 0:128], w1[:, f // 4, j, f % 4 * 128:(f % 4 + 1) * 128],
                                     hT[:, j, :], start=j == 0, stop=j == DB - 1, skip_group_check=True)
                last.then_inc(up_mm, 1)
                if f == 2:
                    pe.wait_ge(*taken(T_MLP - 1))
                if f >= 2:
                    down(f - 2)
            down(F0B - 2)
            down(F0B - 1)
            paths(range(T_MLP, T_NORM3))

            pe.wait_ge(in_small, 80)
            pe.wait_ge(h_ready, 4)
            views = [hn[:, 0:128]] + [hn[:, 128 + m:512:3] for m in range(3)]
            transposes(views, 4, two_banks, hT_ready)
            paths(range(T_NORM3, T_LIFT))
            pe.wait_ge(hT_act, 5)
            pe.wait_ge(hT_dve, 5)
            for j in range(4):
                last = pe.matmul(P[2][:, j * 128:(j + 1) * 128], hT[:, j, :], wup[:, min(j, 1), :], start=True, stop=True)
            last.then_inc(lift_mm, 1)
            paths(range(T_LIFT, EC))
            pe.wait_ge(lift_ready, 1)

            def gather(c, k, first):
                pe.wait_ge(gsel_ready, c + 1)
                if not first:
                    pe.wait_ge(prod_ready, c - UNROLL + 1)
                sel = gsel[c // (EC // 2)][:, c % (EC // 2), :]
                pe.matmul(P[k][:, :], sel, xup_hi[:, :], start=True, stop=False)
                pe.matmul(P[k][:, :], sel, xup_lo[:, :], start=False, stop=True).then_inc(gathered, 1)

            def scatter(c, k):
                p, first, last = prod[k], c == 0, c == EC - 1
                pe.wait_ge(ysel_ready, c + 1)
                pe.wait_ge(prod_ready, c + 1)
                pe.matmul(P[7][:, 0:384], p[:, 0, :], ysel[k][:, :, :].rearrange("p m n -> p (m n)"),
                          start=first, stop=last, skip_group_check=True)
                d = pe.matmul(P[7][:, 384:512], p[:, 5, :], oh[:, c, :].bitcast(f32), start=False, stop=last,
                              skip_group_check=True)
                if last:
                    d.then_inc(bd_done, 1)
                pe.wait_ge(ac_rounded, c + 1)
                pe.matmul(P[6][:, :], oh[:, c, :], ac_hi[k][:, :], start=first, stop=False,
                          skip_group_check=True)
                pe.wait_ge(ac_left, c + 1)
                pe.matmul(P[6][:, :], oh[:, c, :], ac_lo[k][:, :], start=False, stop=last,
                          skip_group_check=True).then_inc(scattered, 1)

            pe.wait_ge(oh_ready, EC)
            for c in range(EC + LAG):
                if c == LAG:
                    pe.wait_ge(*taken(EC - 2))
                    pe.wait_ge(*taken(EC - 1))
                if c < EC:
                    gather(c, c % UNROLL, c < UNROLL)
                if c >= LAG:
                    scatter(c - LAG, (c - LAG) % UNROLL)
            for j in range(4):
                if j % 2 == 0:
                    pe.wait_ge(msg_dve, j // 2 + 1)
                last = pe.transpose(P[0][:, j * 128:(j + 1) * 128], msg[:, j, :], ident[:, :])
            last.then_inc(msgT_mm, 1)
            pe.wait_ge(msgT_act, 2)
            planes = ((7, 1, 0, 0), (4, 2, 1, 3), (5, 2, 2, 3), (6, 2, 3, 3))
            for n, (j, g, _, _) in enumerate(planes):
                pe.matmul(P[2 + n][:, 0:128], msgT[:, j, :], wo[:, g, :], start=True, stop=False)
            pe.wait_ge(msgT_dve, 1)
            for n, (_, _, j, g) in enumerate(planes):
                pe.matmul(P[2 + n][:, 0:128], msgT[:, j, :], wo[:, g, :], start=False, stop=True).then_inc(l1_mm, 1)

            keep_clock(10)
            pe.wait_ge(h_ready, 6)
            for j in range(DB):
                last = pe.matmul(P[j // 2][:, j % 2 * 128:(j % 2 + 1) * 128], hn[:, j * 128:(j + 1) * 128],
                                 cnt_n[:, :], start=True, stop=True)
                if j % 2:
                    last.then_inc(rst_mm, 1)
            pe.transpose(P[7][:, 0:128], adj[:, :], ident[:, :]).then_inc(adjT_mm, 1)
            pe.wait_ge(rst_ready, 2)
            pe.wait_ge(in_l2w1, 16)
            pe.wait_ge(in_l2w2, 16)
            pe.wait_ge(l1_done, 4)

            def down2(j):
                pe.wait_ge(up2_lo, j + 1)
                pe.wait_ge(l2w2_split, j + 1)
                down_block(j, F2B, hid2_hi, hid2_lo, l2w2_hi, l2w2_lo, (3, 6), down2_step, down2_mm)

            for f in range(F2B):
                for j in range(DB):
                    last = pe.matmul(P[(1, 2, 4, 5)[f % 4]][:, 0:128], l2w1[:, j, f * 128:(f + 1) * 128], hT[:, j, :],
                                     start=j == 0, stop=j == DB - 1, skip_group_check=True)
                last.then_inc(up2_mm, 1)
                if f >= 2:
                    down2(f - 2)
            down2(F2B - 2)
            down2(F2B - 1)

            pe.wait_ge(adjT_ready, 1)
            keep_clock(4)
            pe.wait_ge(res_ready, 4)
            for g in range(2):
                pe.matmul(P[5 + g][:, 0:256], ident[:, :], xs[:, g * 256:g * 256 + 256], start=True, stop=False,
                          skip_group_check=True)
            keep_clock(2)
            pe.wait_ge(h_ready, 7)
            transposes(blocks(hn), 4, two_banks, hT_ready)
            keep_clock(3)
            pe.wait_ge(hT_dve, 6)
            pe.wait_ge(hT_act, 6)
            for j in range(DB):
                last = pe.matmul(P[2][:, 0:F3], hT[:, j, :], l3w1[:, j, :], start=j == 0, stop=j == DB - 1)
            last.then_inc(r3_mm, 1)
            keep_clock(3)
            pe.wait_ge(r3_ready, 2)
            pe.matmul(P[4][0:F3 + 1, 0:128], r3[:, :], cnt_ds[:, :], start=True, stop=True).then_inc(z3_mm, 1)
            keep_clock(2)
            pe.wait_ge(z3_ready, 1)
            for g in range(2):
                pe.matmul(P[5 + g][:, 0:256], zT[:, :], l3w2[:, g * 256:g * 256 + 256],
                          start=False, stop=True, skip_group_check=True).then_inc(out_mm, 1)


def kernel(**inputs):
    import numpy as np
    import concourse.bacc as bacc
    from concourse import mybir as _mybir
    from concourse.bass_utils import run_bass_kernel_spmd

    a = {k: np.asarray(v) for k, v in inputs.items()}

    def per_partition(v):
        return v.reshape(-1, 128).T

    def k_major(w):
        return w.reshape(-1, 128, w.shape[1]).transpose(1, 0, 2)

    def twice(w):
        r, c = w.shape
        t = np.zeros((2 * r, 2 * c), w.dtype)
        t[:r, :c] = w
        t[r:, c:] = w
        return t

    b_in = a['L0_gnn_b_in']
    w_in = a['L0_gnn_w_in']
    src, dst = a['src'].astype(np.int32), a['dst'].astype(np.int32)
    y = a['edge_attr_4'].reshape(EC, 128, 4).transpose(1, 0, 2).reshape(128, 4 * EC)
    w2b = np.concatenate([a['L3_gnn_W2'], a['L3_gnn_b2'][None]], 0)
    arrays = {
        'x': a['x'],
        'cols': np.concatenate([per_partition(b_in[:2 * D]), per_partition(b_in[2 * D:]),
                                per_partition(a['L0_gnn_ln1_w']), per_partition(a['L0_gnn_ln1_b']),
                                per_partition(a['L0_gnn_ln2_w']), per_partition(a['L0_gnn_ln2_b']),
                                per_partition(a['L0_gnn_b1']), per_partition(a['L2_gnn_b1']),
                                np.broadcast_to(a['L2_gnn_eps'], (128, 1)), y], 1),
        'idx': np.stack([src.reshape(EC, 128).T, dst.reshape(EC, 128).T], 1),
        'srow': src,
        'feat': np.concatenate([a['edge_attr_8'].reshape(SB, 2, HALF, RB).transpose(1, 3, 0, 2).reshape(2 * RB, SB * HALF),
                                twice(a['L1_gnn_W_mlp1'])], 1),
        'wm23': np.stack([twice(a['L1_gnn_W_mlp2']), twice(a['L1_gnn_W_mlp3'])], 1),
        'w4': np.concatenate([a['L1_gnn_W_mlp4'].reshape(-1, 4, MUL)[:, (1, 0, 2, 3)].reshape(-1, 4 * MUL)] * 2, 0),
        'brow': np.concatenate([a['L0_gnn_b_out'], a['L0_gnn_b2'], a['L2_gnn_b2']]),
        'b31': a['L3_gnn_b1'],
        'wqk': k_major(w_in[:2 * D].T),
        'wv': k_major(w_in[2 * D:].T),
        'wout': k_major(a['L0_gnn_w_out'].T),
        'w1': k_major(a['L0_gnn_w1'].T).reshape(128, DB, 4, 512).transpose(0, 2, 1, 3),
        'w2': k_major(a['L0_gnn_w2'].T),
        'wup': np.stack([a['L1_gnn_W_up0'], a['L1_gnn_W_up1']], 1),
        'wo': np.concatenate([k_major(a['L1_gnn_W_out0']), k_major(a['L1_gnn_W_out1'])], 1),
        'l2w1': k_major(a['L2_gnn_W1']),
        'l2w2': k_major(a['L2_gnn_W2']),
        'l3w1': k_major(a['L3_gnn_W1']),
        'l3w2': w2b,
    }
    arrays = {f"in_{k}": np.ascontiguousarray(v) for k, v in arrays.items()}
    nc = bacc.Bacc("TRN2", target_bir_lowering=False, num_devices=1)
    args = [nc.dram_tensor(k, v.shape, _mybir.dt.from_np(v.dtype), kind="ExternalInput").ap() for k, v in arrays.items()]
    out = nc.dram_tensor("out", (N, D), _mybir.dt.float32, kind="ExternalOutput").ap()
    gnn_stack(nc, *args, out)
    r = run_bass_kernel_spmd(nc, [arrays], core_ids=[0])
    return r.results[0]["out"]
```
